# Optimizing a Trainium2 kernel written in Bass

```python
import numpy as np
import jax
import jax.numpy as jnp

def _softmax(x, axis=-1):
    return jax.nn.softmax(x, axis=axis)
def _gelu(x):
    return jax.nn.gelu(x, approximate=True)
def _silu(x):
    return jax.nn.silu(x)
def _sigmoid(x):
    return jax.nn.sigmoid(x)
def _layernorm(x, axis=-1, eps=1e-5):
    m = jnp.mean(x, axis=axis, keepdims=True)
    v = jnp.var(x, axis=axis, keepdims=True)
    return (x - m) / jnp.sqrt(v + eps)
def _scatter_add(tgt, idx, src, axis=0):
    return tgt.at[idx].add(src)
def _segment_sum(src, seg, n):
    return jax.ops.segment_sum(src, seg, n)

kernel_name = 'mk_adj_preln_d4_adj_128_f530d4'

def setup_inputs(seed: int = 0):
    np.random.seed(seed)
    _w = jnp.asarray
    def _rec_inputs():
        import jax
        import jax.numpy as jnp
        _gk = jax.random.key(seed)
        x = -0.000929 + 1 * jax.random.normal(jax.random.fold_in(_gk, 1), (8192, 128), jnp.float32)
        _a = jax.random.bernoulli(jax.random.fold_in(_gk, 2), 0.000976562, (8192, 8192))
        _a = jnp.logical_or(_a, jnp.swapaxes(_a, -1, -2))
        _a = jnp.logical_or(_a, jnp.eye(8192, dtype=bool))
        adj = _a.astype(jnp.int32)
        return x, adj
    x, adj = _rec_inputs()
    def _L0_gnn_setup():
        import jax, jax.numpy as jnp
        import numpy as np
        N = 8192
        IN_F = 128
        OUT_F = 128
        ALPHA = 0.2
        NEG_INF = -9000000000000000.0
        key = jax.random.key(seed)
        k1, k2, k3, k4, k5 = jax.random.split(key, 5)
        mole_out = jax.random.normal(k1, (N, IN_F), dtype=jnp.float32)
        adj = jax.random.randint(k2, (N, N), 0, 2, dtype=jnp.int32)
        W = jax.random.normal(k3, (IN_F, OUT_F), dtype=jnp.float32) / np.sqrt(IN_F)
        a1 = jax.random.normal(k4, (OUT_F,), dtype=jnp.float32) / np.sqrt(2 * OUT_F)
        a2 = jax.random.normal(k5, (OUT_F,), dtype=jnp.float32) / np.sqrt(2 * OUT_F)
        return {'mole_out': mole_out, 'adj': adj, 'W': W, 'a1': a1, 'a2': a2}
    _L0_gnn_all = _L0_gnn_setup()
    _L0_gnn_in = {k: v for k, v in _L0_gnn_all.items() if k in ('W', 'a1', 'a2', )}
    del _L0_gnn_all

    def _L1_gnn_setup():
        import jax, jax.numpy as jnp
        import numpy as np
        NEG_INF = -9000000000000000.0
        ALPHA = 0.2
        key = jax.random.key(seed)
        k1, k2, k3, k4 = jax.random.split(key, 4)
        N, F_IN, H, D = (8192, 128, 4, 32)
        h = jax.random.normal(k1, (N, F_IN), dtype=jnp.float32)
        adj = jax.random.randint(k2, (N, N), 0, 2, dtype=jnp.int32)
        W = jax.random.normal(k3, (F_IN, H * D), dtype=jnp.float32) * (1.0 / np.sqrt(F_IN))
        a = jax.random.normal(k4, (1, H, 2 * D), dtype=jnp.float32)
        return {'h': h, 'adj': adj, 'W': W, 'a': a}
    _L1_gnn_all = _L1_gnn_setup()
    _L1_gnn_in = {k: v for k, v in _L1_gnn_all.items() if k in ('W', 'a', )}
    del _L1_gnn_all

    def _L2_gnn_setup():
        import jax, jax.numpy as jnp
        import numpy as np
        N = 8192
        IN_F = 128
        OUT_F = 128
        ALPHA = 0.2
        NEG_INF = -9000000000000000.0
        key = jax.random.key(seed)
        k1, k2, k3, k4 = jax.random.split(key, 4)
        h = jax.random.normal(k1, (N, IN_F), dtype=jnp.float32)
        adj = jax.random.randint(k2, (N, N), 0, 2, dtype=jnp.int32)
        W = jax.random.normal(k3, (IN_F, OUT_F), dtype=jnp.float32) * (1.0 / np.sqrt(IN_F))
        limit = 1.414 * np.sqrt(6.0 / (2 * OUT_F + 1))
        a = jax.random.uniform(k4, (2 * OUT_F, 1), dtype=jnp.float32, minval=-limit, maxval=limit)
        return {'h': h, 'adj': adj, 'W': W, 'a': a}
    _L2_gnn_all = _L2_gnn_setup()
    _L2_gnn_in = {k: v for k, v in _L2_gnn_all.items() if k in ('W', 'a', )}
    del _L2_gnn_all

    def _L3_gnn_setup():
        import jax, jax.numpy as jnp
        import numpy as np
        NUM_NODES = 6144
        INPUT_DIM = 128
        OUTPUT_DIM = 128
        NUM_HEADS = 4
        HEAD_DIM = OUTPUT_DIM // NUM_HEADS
        NEG_INF = -9000000000000000.0
        key = jax.random.key(seed)
        k_x, k_adj, k_W, k_a = jax.random.split(key, 4)
        x = jax.random.normal(k_x, (NUM_NODES, INPUT_DIM), dtype=jnp.float32)
        adj = jax.random.randint(k_adj, (NUM_NODES, NUM_NODES), 0, 2, dtype=jnp.int32)
        W = jax.random.uniform(k_W, (NUM_HEADS, INPUT_DIM, HEAD_DIM), dtype=jnp.float32, minval=-1.0, maxval=1.0) * np.sqrt(6.0 / INPUT_DIM)
        a = jax.random.uniform(k_a, (NUM_HEADS, 2 * HEAD_DIM, 1), dtype=jnp.float32, minval=-1.0, maxval=1.0) * np.sqrt(6.0 / (2 * HEAD_DIM))
        return {'x': x, 'adj': adj, 'W': W, 'a': a}
    _L3_gnn_all = _L3_gnn_setup()
    _L3_gnn_in = {k: v for k, v in _L3_gnn_all.items() if k in ('W', 'a', )}
    del _L3_gnn_all

    return {
        "x": x,
        "adj": adj,
        "L0_gnn_W": _L0_gnn_in["W"],
        "L0_gnn_a1": _L0_gnn_in["a1"],
        "L0_gnn_a2": _L0_gnn_in["a2"],
        "L1_gnn_W": _L1_gnn_in["W"],
        "L1_gnn_a": _L1_gnn_in["a"],
        "L2_gnn_W": _L2_gnn_in["W"],
        "L2_gnn_a": _L2_gnn_in["a"],
        "L3_gnn_W": _L3_gnn_in["W"],
        "L3_gnn_a": _L3_gnn_in["a"],
    }

def reference(x, adj, L0_gnn_W, L0_gnn_a1, L0_gnn_a2, L1_gnn_W, L1_gnn_a, L2_gnn_W, L2_gnn_a, L3_gnn_W, L3_gnn_a):
    import jax
    import jax.numpy as jnp
    def _L0_gnn_ref(mole_out, adj, W, a1, a2):
        import jax, jax.numpy as jnp
        import numpy as np
        N = 8192
        IN_F = 128
        OUT_F = 128
        ALPHA = 0.2
        NEG_INF = -9000000000000000.0
        Wh = mole_out @ W
        s1 = Wh @ a1
        s2 = Wh @ a2
        e = jax.nn.leaky_relu(s1[:, None] + s2[None, :], negative_slope=ALPHA)
        att = jnp.where(adj > 0, e, NEG_INF)
        att = jax.nn.softmax(att, axis=1)
        h_prime = att @ Wh
        return jax.nn.elu(h_prime)

    def _L1_gnn_ref(h, adj, W, a):
        import jax, jax.numpy as jnp
        import numpy as np
        NEG_INF = -9000000000000000.0
        ALPHA = 0.2
        N = h.shape[0]
        H = a.shape[1]
        D = a.shape[2] // 2
        Wh = (h @ W).reshape(N, H, D)
        a_src = a[0, :, :D]
        a_dst = a[0, :, D:]
        s_src = jnp.einsum('nhd,hd->nh', Wh, a_src)
        s_dst = jnp.einsum('nhd,hd->nh', Wh, a_dst)
        e = s_src[:, None, :] + s_dst[None, :, :]
        e = jnp.where(e >= 0, e, ALPHA * e)
        e = jnp.where(adj[:, :, None] > 0, e, NEG_INF)
        attention = jax.nn.softmax(e, axis=1)
        h_prime = jnp.einsum('ijh,jhd->ihd', attention, Wh)
        return jax.nn.elu(h_prime.reshape(N, H * D))

    def _L2_gnn_ref(h, adj, W, a):
        import jax, jax.numpy as jnp
        import numpy as np
        N = 8192
        IN_F = 128
        OUT_F = 128
        ALPHA = 0.2
        NEG_INF = -9000000000000000.0
        Wh = h @ W
        a1 = a[:OUT_F, 0]
        a2 = a[OUT_F:, 0]
        s1 = Wh @ a1
        s2 = Wh @ a2
        e = jax.nn.leaky_relu(s1[:, None] + s2[None, :], negative_slope=ALPHA)
        masked = jnp.where(adj > 0, e, NEG_INF)
        attention = jax.nn.softmax(masked, axis=1)
        h_prime = attention @ Wh
        return jax.nn.elu(h_prime)

    def _L3_gnn_ref(x, adj, W, a):
        import jax, jax.numpy as jnp
        import numpy as np
        NUM_NODES = 6144
        INPUT_DIM = 128
        OUTPUT_DIM = 128
        NUM_HEADS = 4
        HEAD_DIM = OUTPUT_DIM // NUM_HEADS
        NEG_INF = -9000000000000000.0
        H, Din, d = W.shape
        N = x.shape[0]
        h = jnp.einsum('ni,hid->hnd', x, W)
        a_dst = a[:, :d, 0]
        a_src = a[:, d:, 0]
        s_dst = jnp.einsum('hnd,hd->hn', h, a_dst)
        s_src = jnp.einsum('hnd,hd->hn', h, a_src)
        energy = jax.nn.leaky_relu(s_src[:, :, None] + s_dst[:, None, :], negative_slope=0.2)
        energy = jnp.where(adj[None] > 0, energy, NEG_INF)
        attention = jax.nn.softmax(energy, axis=-1)
        h_prime = jnp.einsum('hij,hjd->hid', attention, h)
        return jnp.reshape(h_prime, (N, H * d))

    h = jnp.maximum(_layernorm(x, axis=-1), 0.0)
    x = x + _L0_gnn_ref(h, adj, L0_gnn_W, L0_gnn_a1, L0_gnn_a2)
    h = jnp.maximum(_layernorm(x, axis=-1), 0.0)
    x = x + _L1_gnn_ref(h, adj, L1_gnn_W, L1_gnn_a)
    h = jnp.maximum(_layernorm(x, axis=-1), 0.0)
    x = x + _L2_gnn_ref(h, adj, L2_gnn_W, L2_gnn_a)
    h = jnp.maximum(_layernorm(x, axis=-1), 0.0)
    x = x + _L3_gnn_ref(h, adj, L3_gnn_W, L3_gnn_a)
    return x


_drawn_inputs = setup_inputs


def setup_inputs(seed=0):
    import zlib

    import numpy as np

    out = dict(_drawn_inputs(seed))
    spreads = {}
    factors = {}
    for name, (base, spread) in spreads.items():
        noise = np.random.default_rng([zlib.crc32(name.encode()), seed]).standard_normal(out[name].shape)
        drawn = base * np.exp(spread * noise) if base else spread * noise
        out[name] = jnp.asarray(drawn.astype(out[name].dtype))
    for name, factor in factors.items():
        out[name] = (out[name] * factor).astype(out[name].dtype)
    return out
```

```python
import math
from contextlib import ExitStack, contextmanager

import concourse.bass as bass
from concourse import mybir

F32 = mybir.dt.float32
BF16 = mybir.dt.bfloat16
I32 = mybir.dt.int32
ALU = mybir.AluOpType
ACT = mybir.ActivationFunctionType
AX = mybir.AxisListType
RMAX = bass.bass_isa.ReduceOp.max

P = 128
N = 8192
F = 128
T = N // P
ALPHA = 0.2
EPS = 1e-5
BANK = 512
PIECES = 3
IBLK = 512
NEG_INF = -9000000000000000.0
WIDEST = 60.0
TINY = 2.0 ** -60


class Kind:

    def __init__(self, heads, width, pass_heads, passes, rows, load_tiles, step_tiles):
        self.heads, self.width, self.pass_heads, self.passes = heads, width, pass_heads, passes
        self.rows, self.load_tiles, self.step_tiles = rows, load_tiles, step_tiles


class Guarded:

    def __init__(self, sync, scalar, vector, tensor, gpsimd):
        self.sync, self.scalar, self.vector, self.tensor, self.gpsimd = sync, scalar, vector, tensor, gpsimd


class Shared:
    pass


ONE_HEAD = Kind(
    heads=1, width=F + 1,
    pass_heads=1, passes=1,
    rows=512,
    load_tiles=8,
    step_tiles=4,
)
FOUR_HEADS = Kind(
    heads=4, width=F // 4 + 1, pass_heads=2, passes=2, rows=1024, load_tiles=4, step_tiles=1,
)
KINDS = [ONE_HEAD, FOUR_HEADS, ONE_HEAD, FOUR_HEADS]
ROW_MAX = max(k.heads * k.width for k in KINDS)
STAT_MAX = max(2 * k.heads * PIECES * k.width for k in KINDS)
AUG = F + 2 * 4


def guarded(block, go):
    if go is None:
        return block

    def only_if(attach):
        def take(program):
            def body(engine):
                with engine.If(go > 0):
                    program(engine)
                with engine.Else():
                    engine.nop()

            attach(body)

        return take

    return Guarded(sync=only_if(block.sync), scalar=only_if(block.scalar), vector=only_if(block.vector),
                           tensor=only_if(block.tensor), gpsimd=only_if(block.gpsimd))


@contextmanager
def stage_semaphores(nc, tag):
    with ExitStack() as st:
        made = []

        def sem(name):
            made.append(st.enter_context(nc.semaphore(f"{tag}_{name}")))
            return made[-1]

        yield sem
        with nc.Block() as block:

            @block.gpsimd
            def _(pool):
                for s in made:
                    pool.sem_clear(s)


def tensors(nc, ctx):
    def sb(name, shape, dt):
        return ctx.enter_context(nc.sbuf_tensor(name, shape, dt))

    g = Shared()
    g.identf = sb("identf", [P, P], F32)
    g.identb = sb("identb", [P, P], BF16)
    g.zeros = sb("zeros", [P, P], BF16)
    g.onesf = sb("onesf", [P, P], F32)
    g.waug = sb("waug", [P, 4, AUG], F32)
    g.widest = sb("widest", [P, 1], F32)
    g.exact = sb("exact", [P, 1], I32)
    g.score = sb("score", [P, T * 4], F32)
    g.ra = sb("ra", [P, T * 4], F32)
    g.rb = sb("rb", [P, T * 4], F32)
    g.colsum = sb("colsum", [P, ROW_MAX], F32)
    g.adj_t = nc.dram_tensor("adj_t", [N // IBLK, P, T, IBLK], BF16, kind="Internal").ap()
    g.scores = nc.dram_tensor("scores", [2, 4, T, P], F32, kind="Internal").ap()
    g.values = nc.dram_tensor("values", [P, T * ROW_MAX], F32, kind="Internal").ap()
    g.nodes = nc.dram_tensor("nodes", [N, F], F32, kind="Internal").ap()
    g.rows1 = nc.dram_tensor("rows1", [4, N], F32, kind="Internal").ap()
    g.sums = [nc.dram_tensor(f"sums{l}", [T, P, k.heads * k.width] if l < 3 else [k.heads, N, k.width], F32,
                             kind="Internal").ap() for l, k in enumerate(KINDS)]
    g.pool_stored = ctx.enter_context(nc.semaphore("pool_stored"))
    g.pool_stores = 0
    return g


def setup(nc, sem, g, weights):
    blank, weights_in, made, summed = sem("blank"), sem("weights_in"), sem("made"), sem("summed")
    with ExitStack() as st:
        vecs = st.enter_context(nc.sbuf_tensor("vecs", [P, 4, 2, F], F32))
        prod = st.enter_context(nc.sbuf_tensor("prod", [P, 4, 2, F], F32))
        with nc.Block() as block:

            @block.sync
            def _(sp):
                for l, (w, score_i, score_j) in enumerate(weights):
                    if len(w.shape) == 3:
                        dst = g.waug[:, l, 0:F].rearrange("p (h d) -> p h d", h=w.shape[0])
                        sp.dma_start(dst, w.rearrange("h p d -> p h d")).then_inc(weights_in, 16)
                    else:
                        sp.dma_start(g.waug[:, l, 0:F], w).then_inc(weights_in, 16)
                    for k, a in enumerate((score_i, score_j)):
                        h, d = a.shape
                        dst = vecs[:, l, k, :].rearrange("p (h d) -> p h d", h=h)
                        sp.dma_start(dst, a.unsqueeze(0).broadcast_to([P, h, d])).then_inc(weights_in, 16)

            @block.gpsimd
            def _(pool):
                nc.gpsimd.memset(g.identf[:, :], 0.0).then_inc(blank, 1)
                nc.gpsimd.memset(g.identb[:, :], 0.0).then_inc(blank, 1)
                nc.gpsimd.memset(g.zeros[:, :], 0.0).then_inc(blank, 1)
                nc.gpsimd.memset(g.onesf[:, :], 1.0).then_inc(blank, 1)
                nc.gpsimd.memset(g.widest[:, :], 0.0)
                pool.wait_ge(blank, 4)
                for m in (g.identf, g.identb):
                    nc.gpsimd.affine_select(out=m[:, :], in_=m[:, :], compare_op=ALU.not_equal, fill=1.0,
                                            base=0, pattern=[[-1, P]], channel_multiplier=1).then_inc(blank, 1)

            @block.vector
            def _(dve):
                dve.wait_ge(weights_in, 16 * 12)
                for l in range(4):
                    nc.vector.tensor_tensor(prod[:, l], vecs[:, l],
                                            g.waug[:, l, 0:F].unsqueeze(1).broadcast_to([P, 2, F]),
                                            ALU.mult).then_inc(made, 1)
                dve.wait_ge(made, 4)
                for l, k in enumerate(KINDS):
                    dst = g.waug[:, l, F:F + 2 * k.heads].rearrange("p (k h) -> p k h", k=2)
                    src = prod[:, l].rearrange("p k (h d) -> p k h d", h=k.heads)
                    nc.vector.tensor_reduce(dst, src, AX.X, ALU.add).then_inc(summed, 1)


def transpose_adjacency(nc, sem, g, adj):
    COLS = 1024
    NT, NI = COLS // P, IBLK // P
    ITEMS = N // COLS
    int_in, int_used, ones_ready = [sem("int_in0"), sem("int_in1")], sem("int_used"), sem("ones_ready")
    turned, bank_free, packed = sem("turned"), sem("bank_free"), sem("packed")
    stored, out_free = [sem("stored0"), sem("stored1")], sem("out_free")
    with ExitStack() as st:
        raw = [st.enter_context(nc.sbuf_tensor(f"raw{b}", [P, NI, COLS], I32)) for b in range(2)]
        ones = [st.enter_context(nc.sbuf_tensor(f"ones{b}", [P, NI, COLS], BF16)) for b in range(2)]
        pack = [st.enter_context(nc.sbuf_tensor(f"pack{b}", [P, NT, IBLK], BF16)) for b in range(2)]
        turn = st.enter_context(nc.psum_tensor("turn", [P, 8, 2, IBLK], BF16))
        BANKS = NT // 2
        with nc.Block() as block:

            @block.sync
            def _(sp):
                with sp.Fori(0, N // IBLK) as ib:
                    with sp.Fori(0, ITEMS // 2) as jj:
                        for b in range(2):
                            n = (ib * (ITEMS // 2) + jj) * 2 + b
                            sp.wait_ge(int_used, n + 1)
                            src = adj[bass.ds(ib * IBLK, IBLK), bass.ds((jj * 2 + b) * COLS, COLS)]
                            sp.dma_start(raw[b][:, :, :], src.rearrange("(t p) c -> p t c", p=P)).then_inc(int_in[b], 16)

            @block.vector
            def _(dve):
                dve.sem_inc(int_used, 2)
                with dve.Fori(0, N // IBLK * ITEMS // 2) as jj:
                    for b in range(2):
                        n = jj * 2 + b
                        dve.wait_ge(int_in[b], (jj + 1) * 16)
                        dve.wait_ge(turned, n + 1)
                        nc.vector.tensor_scalar(ones[b][:, :, :], raw[b][:, :, :], 0, None,
                                                ALU.is_gt).then_inc(int_used, 1)

            @block.tensor
            def _(pe):
                pe.sem_inc(turned, 2)
                with pe.Fori(0, N // IBLK * ITEMS // 2) as jj:
                    for b in range(2):
                        n = jj * 2 + b
                        pe.wait_ge(int_used, n + 3)
                        for k in range(BANKS):
                            pe.wait_ge(bank_free, (n * BANKS + k) + 1)
                            for t in range(2 * k, 2 * k + 2):
                                for i in range(NI):
                                    last = nc.tensor.transpose(turn[:, b * BANKS + k, t % 2, i * P:(i + 1) * P],
                                                               ones[b][:, i, t * P:(t + 1) * P], g.identb[:, :])
                            if k < BANKS - 1:
                                last.then_inc(packed, 1)
                        last.then_inc(turned, 1)

            @block.scalar
            def _(act):
                act.sem_inc(bank_free, 8)
                with act.Fori(0, N // IBLK) as ib:
                    with act.Fori(0, ITEMS // 2) as jj:
                        for b in range(2):
                            n = (ib * (ITEMS // 2) + jj) * 2 + b
                            act.wait_ge(out_free, n + 1)
                            for k in range(BANKS):
                                if k < BANKS - 1:
                                    act.wait_ge(packed, n * (BANKS - 1) + k + 1)
                                else:
                                    act.wait_ge(turned, n + 3)
                                last = nc.scalar.activation(pack[b][:, 2 * k:2 * k + 2, :], turn[:, b * BANKS + k],
                                                            ACT.Copy)
                                last.then_inc(bank_free, 1)
                            act.wait_ge(bank_free, (n + 1) * BANKS + 8)
                            dst = g.adj_t[bass.ds(ib, 1), :, bass.ds((jj * 2 + b) * NT, NT), :]
                            act.dma_start(dst.rearrange("b p t i -> (b p) t i"), pack[b][:, :, :]).then_inc(stored[b], 16)

            @block.gpsimd
            def _(pool):
                pool.sem_inc(out_free, 2)
                with pool.Fori(0, N // IBLK * ITEMS // 2) as jj:
                    for b in range(2):
                        pool.wait_ge(stored[b], (jj + 1) * 16)
                        pool.sem_inc(out_free, 1)


def update_nodes(nc, sem, g, layer, x_in, out, go=None):
    before = KINDS[layer - 1] if layer else None
    kind = KINDS[layer] if layer < 4 else None
    elu = layer < 4
    tag = f"{layer}" if go is None else f"{layer}x"
    PART = 8
    PARTS = T // PART
    with ExitStack() as st:
        def sb(name, shape, dt=F32):
            return st.enter_context(nc.sbuf_tensor(f"{name}_{tag}", shape, dt))

        x = sb("x", [P, T, F])
        vals = sb("vals", [P, T * ROW_MAX])
        stats = sb("stats", [P, PART, 6])
        pair = sb("pair", [P, PART, 2])
        mv = sb("mv", [P, T, 2])
        rstd = sb("rstd", [P, T])
        x_landed, s_landed = sem("x_landed"), sem("s_landed")
        chain, low, raised, x_ready, measured = sem("chain"), sem("low"), sem("raised"), sem("x_ready"), sem("measured")
        stood = sem("stood")
        x_src = x_in if layer < 2 else g.nodes
        with ExitStack() as st1:
            frac = st1.enter_context(nc.sbuf_tensor(f"frac_{tag}", [P, PART, F], F32))
            expm = st1.enter_context(nc.sbuf_tensor(f"expm_{tag}", [P, PART * F], F32))
            rden = st1.enter_context(nc.sbuf_tensor(f"rden_{tag}", [P, PART * 4], F32))
            with nc.Block() as plain:
                block = guarded(plain, go)

                @block.sync
                def _(sp):
                    HALVES = PARTS // 4 if layer == 4 else PARTS
                    with sp.Fori(0, PARTS // HALVES) as head:
                        with sp.Fori(0, HALVES) as half:
                            p = head * HALVES + half
                            rows = x_src[bass.ds(p * (PART * P), PART * P), :].rearrange("(t p) f -> p t f", p=P)
                            sp.dma_start(x[:, bass.ds(p * PART, PART), :], rows).then_inc(x_landed, 16)
                            if before:
                                row = before.heads * before.width
                                if layer < 4:
                                    src = g.sums[layer - 1][bass.ds(p * PART, PART)].rearrange("t p w -> p t w")
                                else:
                                    src = g.sums[3][bass.ds(head, 1), bass.ds(half * (PART * P * 4), PART * P * 4), :]
                                    src = src.rearrange("a (t p i) w -> p (a t) (i w)", p=P, i=4)
                                dst = vals[:, bass.ds(p * (PART * row), PART * row)]
                                sp.dma_start(dst.rearrange("p (t w) -> p t w", t=PART), src).then_inc(s_landed, 16)
                                sp.wait_ge(s_landed, (p + 1) * 16)
                            sp.wait_ge(x_landed, (p + 1) * 16)
                            sp.sem_inc(stood, 1)

                @block.gpsimd
                def _(pool):
                    if before:
                        dst = out if layer == 4 else g.nodes
                        with pool.Fori(0, PARTS) as p:
                            pool.wait_ge(x_ready, p + 1)
                            rows = dst[bass.ds(p * (PART * P), PART * P), :].rearrange("(t p) f -> p t f", p=P)
                            pool.dma_start(rows, x[:, bass.ds(p * PART, PART), :]).then_inc(g.pool_stored, 16)
                        g.pool_stores += 16 * PARTS
                        pool.wait_ge(g.pool_stored, g.pool_stores)

                @block.scalar
                def _(act):
                    if before and elu:
                        with act.Fori(0, PARTS) as p:
                            act.wait_ge(low, p + 1)
                            nc.scalar.activation(expm[:, :], expm[:, :], ACT.Exp).then_inc(raised, 1)

                @block.vector
                def _(dve):
                    LINKS = (3 if elu else 2) if before else 0
                    with dve.Fori(0, PARTS) as p:
                        made = [0]

                        def link(ins):
                            made[0] += 1
                            ins.then_inc(chain, 1)
                            dve.wait_ge(chain, p * LINKS + made[0])

                        xp = x[:, bass.ds(p * PART, PART), :]
                        dve.wait_ge(x_landed, (p + 1) * 16)
                        if before:
                            H, W = before.heads, before.width
                            s = vals[:, bass.ds(p * (PART * H * W), PART * H * W)]
                            s = s.rearrange("p (u w) -> p u w", w=W)
                            dve.wait_ge(s_landed, (p + 1) * 16)
                            link(nc.vector.reciprocal(rden[:, 0:PART * H], s[:, :, W - 1]))
                            f = frac[:, :, :].rearrange("p t (h d) -> p (t h) d", h=H)
                            link(nc.vector.tensor_tensor(
                                f, s[:, :, 0:W - 1],
                                rden[:, 0:PART * H].unsqueeze(2).broadcast_to([P, PART * H, W - 1]), ALU.mult))
                            flat = frac[:, :, :].rearrange("p t f -> p (t f)")
                            if elu:
                                nc.vector.tensor_scalar(expm[:, :], flat, 0.0, None, ALU.min).then_inc(low, 1)
                                dve.wait_ge(raised, p + 1)
                                link(nc.vector.scalar_tensor_tensor(expm[:, :], flat, 0.0, expm[:, :],
                                                                    ALU.max, ALU.add))
                                nc.vector.scalar_tensor_tensor(xp, expm[:, :].rearrange("p (t f) -> p t f", f=F), -1.0,
                                                               xp, ALU.add, ALU.add).then_inc(x_ready, 1)
                            else:
                                nc.vector.tensor_tensor(xp, frac[:, :, :], xp, ALU.add).then_inc(x_ready, 1)
                            dve.wait_ge(x_ready, p + 1)
                        if kind:
                            dve.sem_inc(stood, 1)
                            for t in range(PART):
                                last = nc.vector.bn_stats(stats[:, t, :], x[:, bass.ds(p * PART + t, 1), :]
                                                          .rearrange("p a f -> p (a f)"))
                            last.then_inc(measured, 1)
                            dve.wait_ge(measured, 3 * p + 1)
                            dve.sem_inc(stood, 1)
                            for t in range(PART):
                                last = nc.vector.bn_aggr(pair[:, t, :], stats[:, t, :])
                            last.then_inc(measured, 1)
                            dve.wait_ge(measured, 3 * p + 2)
                            nc.vector.tensor_copy(mv[:, bass.ds(p * PART, PART), :], pair[:, :, :]).then_inc(measured, 1)
                            dve.wait_ge(measured, 3 * p + 3)
        if not kind:
            return
        H, W = kind.heads, kind.width
        ROW = H * W
        CH = 4
        CHUNKS = T // CH
        cols = F + 2 * H
        scol = sb("scol", [P, T, 2 * H])
        with ExitStack() as st2:
            hn = [st2.enter_context(nc.sbuf_tensor(f"hn{b}_{tag}", [P, CH, F], F32)) for b in range(2)]
            ht = [st2.enter_context(nc.sbuf_tensor(f"ht{b}_{tag}", [P, CH * P], F32)) for b in range(2)]
            srow = [st2.enter_context(nc.sbuf_tensor(f"srow{b}_{tag}", [H, CH * P], F32)) for b in range(2)]
            pt = [st2.enter_context(nc.psum_tensor(f"pt{b}_{tag}", [P, CH * P], F32)) for b in range(2)]
            pv = [st2.enter_context(nc.psum_tensor(f"pv{b}_{tag}", [P, 2, BANK], F32)) for b in range(2)]
            ps = [st2.enter_context(nc.psum_tensor(f"ps{b}_{tag}", [P, BANK], F32)) for b in range(2)]
            rooted, inverse = sem("rooted"), sem("inverse")
            h_ready, turned, ht_ready, projected = sem("h_ready"), sem("turned"), sem("ht_ready"), sem("projected")
            v_copied, row_made, row_ready = sem("v_copied"), sem("row_made"), sem("row_ready")
            row_out, row_free, ones_set = sem("row_out"), sem("row_free"), sem("ones_set")
            with nc.Block() as plain:
                block = guarded(plain, go)

                @block.gpsimd
                def _(pool):
                    u = vals[:, 0:T * ROW].rearrange("p (u w) -> p u w", w=W)
                    nc.gpsimd.memset(u[:, :, W - 1], 1.0).then_inc(ones_set, 1)

                @block.sync
                def _(sp):
                    sp.sem_inc(row_free, 2)
                    with sp.Fori(0, CHUNKS // 2) as cc:
                        for b in range(2):
                            c = cc * 2 + b
                            sp.wait_ge(row_ready, c + 1)
                            sp.dma_start(g.rows1[0:H, bass.ds(c * (CH * P), CH * P)], srow[b][:, :]).then_inc(row_out, 16)
                            sp.wait_ge(row_out, (c + 1) * 16)
                            sp.sem_inc(row_free, 1)

                @block.vector
                def _(dve):
                    nc.vector.tensor_scalar(rstd[:, :], mv[:, :, 1], EPS, None, ALU.add).then_inc(rooted, 1)
                    dve.wait_ge(rooted, 2)
                    nc.vector.reciprocal(rstd[:, :], rstd[:, :]).then_inc(inverse, 1)
                    dve.wait_ge(inverse, 1)
                    dve.sem_inc(row_made, 2)
                    with dve.Fori(0, CHUNKS // 2) as cc:
                        for b in range(2):
                            c = cc * 2 + b
                            dve.wait_ge(turned, c + 1)
                            for t in range(CH):
                                tile = bass.ds(c * CH + t, 1)
                                last = nc.vector.tensor_scalar(
                                    hn[b][:, t, :], x[:, tile, :].rearrange("p a f -> p (a f)"),
                                    mv[:, tile, 0:1].rearrange("p a f -> p (a f)"), rstd[:, tile],
                                    ALU.subtract, ALU.mult)
                            last.then_inc(h_ready, 1)
                            dve.wait_ge(projected, c + 1)
                            dve.wait_ge(row_free, c + 1)
                            nc.vector.tensor_scalar(srow[b][:, :], ps[b][0:H, :], TINY, None, ALU.add).then_inc(row_made, 1)
                            dve.wait_ge(row_made, c + 3)
                            bits = srow[b][:, :].bitcast(I32)
                            nc.vector.tensor_scalar(bits, bits, 1, None, ALU.bitwise_or).then_inc(row_ready, 1)

                @block.tensor
                def _(pe):
                    pe.sem_inc(turned, 2)
                    with pe.Fori(0, CHUNKS // 2) as cc:
                        for b in range(2):
                            c = cc * 2 + b
                            pe.wait_ge(h_ready, c + 1)
                            pe.wait_ge(ht_ready, c + 1)
                            for t in range(CH):
                                last = nc.tensor.transpose(pt[b][:, t * P:(t + 1) * P], hn[b][:, t, :], g.identf[:, :])
                            last.then_inc(turned, 1)
                            pe.wait_ge(ht_ready, c + 3)
                            pe.wait_ge(v_copied, c + 1)
                            pe.wait_ge(row_made, c + 1)
                            for t in range(CH):
                                nc.tensor.matmul(pv[b][:, t // 2, (t % 2) * cols:(t % 2 + 1) * cols],
                                                 ht[b][:, t * P:(t + 1) * P], g.waug[:, layer, 0:cols],
                                                 start=True, stop=True)
                            nc.tensor.matmul(ps[b][0:H, :], g.waug[:, layer, F:F + H], ht[b][:, :],
                                             start=True, stop=True).then_inc(projected, 1)

                @block.scalar
                def _(act):
                    act.wait_ge(rooted, 1)
                    nc.scalar.activation(rstd[:, :], rstd[:, :], ACT.Sqrt).then_inc(rooted, 1)
                    act.sem_inc(ht_ready, 2)
                    act.sem_inc(v_copied, 2)
                    with act.Fori(0, CHUNKS // 2) as cc:
                        for b in range(2):
                            c = cc * 2 + b
                            act.wait_ge(turned, c + 3)
                            nc.scalar.activation(ht[b][:, :], pt[b][:, :], ACT.Relu).then_inc(ht_ready, 1)
                            act.wait_ge(projected, c + 1)
                            for k in range(2):
                                src = pv[b][:, k, 0:2 * cols].rearrange("p (t c) -> p t c", c=cols)[:, :, F:cols]
                                nc.scalar.activation(scol[:, bass.ds(c * CH + 2 * k, 2), :], src, ACT.Copy)
                                dst = vals[:, bass.ds((c * CH + 2 * k) * ROW, 2 * ROW)]
                                dst = dst.rearrange("p (t h w) -> p t h w", t=2, h=H)[:, :, :, 0:W - 1]
                                src = pv[b][:, k, 0:2 * cols].rearrange("p (t c) -> p t c", c=cols)[:, :, 0:F]
                                src = src.rearrange("p t (h d) -> p t h d", h=H)
                                last = nc.scalar.activation(dst, src, ACT.Copy)
                            last.then_inc(v_copied, 1)

        if go is not None:
            store_for_exact(nc, sem, g, kind, scol, vals, go)
            return

        with ExitStack() as st3:
            def sb3(name, shape, dt=F32):
                return st3.enter_context(nc.sbuf_tensor(f"{name}_{tag}", shape, dt))

            ends, most = sb3("ends", [P, 2 * H]), sb3("most", [P, 2 * H])
            tlow, thigh, u = sb3("tlow", [P, T, H]), sb3("thigh", [P, T, H]), sb3("u", [P, T, H])
            col = [sb3("ca", [P, T, H]), sb3("cb", [P, T, H])]
            UT = 4
            whole = [sb3(f"whole{b}", [P, UT * ROW]) for b in range(2)]
            rest = [sb3(f"rest{b}", [P, UT * ROW]) for b in range(2)]
            ptot = st3.enter_context(nc.psum_tensor(f"ptot_{tag}", [P, BANK], F32))
            UNITS = T // UT * 2
            ends_ready, most_ready, spread, exps = sem("ends_ready"), sem("most_ready"), sem("spread"), sem("exps")
            totalled, ranged = sem("totalled"), sem("ranged")
            wholes, highs, rests, mids, lows = sem("wholes"), sem("highs"), sem("rests"), sem("mids"), sem("lows")
            pieces = g.split[:, 0:T * 2 * PIECES * ROW].rearrange("p (t h s q w) -> p t h s q w", t=T, h=H, s=2, q=PIECES)

            def piece(cc, side, q):
                v = pieces[:, bass.ds(cc * UT, UT), :, side, q, :]
                return v

            def unit(buf):
                return buf[:, :].rearrange("p (t h w) -> p t h w", t=UT, h=H)

            with nc.Block() as plain:
                block = guarded(plain, go)

                @block.gpsimd
                def _(pool):
                    pool.wait_ge(ends_ready, 2)
                    nc.gpsimd.partition_all_reduce(most[:, :], ends[:, :], P, RMAX).then_inc(most_ready, 1)
                    pool.wait_ge(exps, 2)
                    with pool.Fori(0, T // UT) as cc:
                        for side in range(2):
                            pool.wait_ge(rests, cc * 2 + side + 1)
                            v = vals[:, bass.ds(cc * (UT * ROW), UT * ROW)].rearrange("p (t h w) -> p t h w", t=UT, h=H)
                            c = col[side][:, bass.ds(cc * UT, UT), :].unsqueeze(3).broadcast_to([P, UT, H, W])
                            nc.gpsimd.tensor_tensor(unit(whole[side]), v, c, ALU.mult).then_inc(wholes, 1)

                @block.tensor
                def _(pe):
                    nc.tensor.matmul(ptot[:, 0:ROW], g.onesf[:, :], vals[:, 0:ROW], start=True, stop=False)
                    with pe.Fori(1, T - 1) as t:
                        nc.tensor.matmul(ptot[:, 0:ROW], g.onesf[:, :], vals[:, bass.ds(t * ROW, ROW)],
                                         start=False, stop=False)
                    nc.tensor.matmul(ptot[:, 0:ROW], g.onesf[:, :], vals[:, (T - 1) * ROW:T * ROW],
                                     start=False, stop=True).then_inc(totalled, 1)

                @block.scalar
                def _(act):
                    act.wait_ge(spread, 2)
                    nc.scalar.activation(col[0][:, :, :], u[:, :, :], ACT.Exp).then_inc(exps, 1)
                    nc.scalar.activation(col[1][:, :, :], u[:, :, :], ACT.Exp, scale=ALPHA).then_inc(exps, 1)
                    act.wait_ge(spread, 4)
                    nc.scalar.activation(g.ra[:, 0:T * H], tlow[:, :, :].rearrange("p t h -> p (t h)"), ACT.Exp,
                                         scale=1 - ALPHA).then_inc(exps, 1)
                    nc.scalar.activation(g.rb[:, 0:T * H], thigh[:, :, :].rearrange("p t h -> p (t h)"), ACT.Exp,
                                         scale=ALPHA - 1).then_inc(exps, 1)
                    with act.Fori(0, T // UT) as cc:
                        for side in range(2):
                            n = cc * 2 + side
                            act.wait_ge(wholes, n + 1)
                            nc.scalar.activation(piece(cc, side, 0), unit(whole[side]), ACT.Copy).then_inc(highs, 1)
                            act.wait_ge(rests, n + 3)
                            nc.scalar.activation(piece(cc, side, 1), unit(rest[side]), ACT.Copy).then_inc(mids, 1)

                @block.vector
                def _(dve):
                    dve.sem_inc(rests, 2)
                    s2 = scol[:, :, H:2 * H]
                    nc.vector.tensor_reduce(ends[:, 0:H], s2.rearrange("p t h -> p h t"), AX.X, ALU.max).then_inc(ends_ready, 1)
                    nc.vector.tensor_reduce(ends[:, H:2 * H], s2.rearrange("p t h -> p h t"), AX.X, ALU.min,
                                            negate=True).then_inc(ends_ready, 1)
                    dve.wait_ge(most_ready, 1)
                    nc.vector.tensor_tensor(ends[:, 0:H], most[:, 0:H], most[:, H:2 * H], ALU.add).then_inc(ranged, 1)
                    dve.wait_ge(ranged, 1)
                    nc.vector.tensor_reduce(ends[:, H:H + 1], ends[:, 0:H], AX.X, ALU.max).then_inc(ranged, 1)
                    dve.wait_ge(ranged, 2)
                    nc.vector.tensor_tensor(g.widest[:, :], g.widest[:, :], ends[:, H:H + 1], ALU.max)
                    top = most[:, 0:H].unsqueeze(1).broadcast_to([P, T, H])
                    nc.vector.tensor_tensor(u[:, :, :], s2, top, ALU.subtract).then_inc(spread, 1)
                    nc.vector.tensor_tensor(thigh[:, :, :], scol[:, :, 0:H], top, ALU.add).then_inc(spread, 1)
                    dve.wait_ge(spread, 2)
                    nc.vector.tensor_scalar(tlow[:, :, :], thigh[:, :, :], 0.0, None, ALU.min).then_inc(spread, 1)
                    dve.wait_ge(spread, 3)
                    nc.vector.tensor_scalar(thigh[:, :, :], thigh[:, :, :], 0.0, None, ALU.max).then_inc(spread, 1)
                    nc.vector.tensor_scalar(g.score[:, 0:T * H].rearrange("p (t h) -> p t h", h=H).bitcast(I32),
                                            s2.bitcast(I32), -2, None, ALU.bitwise_and).then_inc(ends_ready, 1)
                    dve.wait_ge(totalled, 1)
                    nc.vector.tensor_copy(g.colsum[:, 0:ROW], ptot[:, 0:ROW]).then_inc(ends_ready, 1)
                    with dve.Fori(0, T // UT) as cc:
                        for side in range(2):
                            n = cc * 2 + side
                            dve.wait_ge(highs, n + 1)
                            dve.wait_ge(wholes, n + 1)
                            nc.vector.tensor_tensor(unit(rest[side]), unit(whole[side]), piece(cc, side, 0),
                                                    ALU.subtract).then_inc(rests, 1)
                            dve.wait_ge(mids, n + 1)
                            nc.vector.tensor_tensor(piece(cc, side, 2), unit(rest[side]), piece(cc, side, 1),
                                                    ALU.subtract).then_inc(lows, 1)
                            dve.wait_ge(lows, n + 1)


def store_for_exact(nc, sem, g, kind, scol, vals, go):
    H, ROW = kind.heads, kind.heads * kind.width
    saved = sem("saved")
    with nc.Block() as plain:
        block = guarded(plain, go)

        @block.sync
        def _(sp):
            for k in range(2):
                for h in range(H):
                    sp.dma_start(g.scores[k, h].rearrange("t p -> p t"), scol[:, :, k * H + h]).then_inc(saved, 16)
            sp.dma_start(g.values[:, 0:T * ROW], vals[:, 0:T * ROW]).then_inc(saved, 16)
            sp.wait_ge(saved, 16 * (2 * H + 1))


def decide(nc, sem, g):
    decided = sem("decided")
    with nc.Block() as block:

        @block.vector
        def _(dve):
            nc.vector.tensor_scalar(g.exact[:, :], g.widest[:, :], WIDEST, None, ALU.is_gt).then_inc(decided, 1)
            dve.wait_ge(decided, 1)


def attend_exact(nc, sem, g, layer, adj, go):
    kind = KINDS[layer]
    H, W = kind.heads, kind.width
    ROW = H * W
    GROUP = 4
    GROUPS = T // GROUP
    LINKS = 6
    adj_in, vals_in, row_in, row_used, shifted = sem("adj_in"), sem("vals_in"), sem("row_in"), sem("row_used"), sem("shifted")
    raised, turned, copied, added = sem("raised"), sem("turned"), sem("copied"), sem("added")
    summed, held, sums_out, chain, stood = sem("summed"), sem("held"), sem("sums_out"), sem("chain"), sem("stood")
    res_free = sem("res_free")
    with ExitStack() as st:
        def sb(name, shape, dt=F32):
            return st.enter_context(nc.sbuf_tensor(f"x{name}_{layer}", shape, dt))

        ints = sb("ints", [P, N], I32)
        edge = sb("edge", [P, N])
        row = sb("row", [P, N])
        e = sb("e", [P, N])
        s1 = sb("s1", [P, H, T])
        vals = sb("vals", [P, T * ROW])
        top, ntop = sb("top", [P, 1]), sb("ntop", [P, 1])
        pt = [sb(f"pt{b}", [P, GROUP * P]) for b in range(2)]
        res = sb("res", [P, W])
        turn = [st.enter_context(nc.psum_tensor(f"xturn{b}_{layer}", [P, GROUP * P], F32)) for b in range(2)]
        acc = st.enter_context(nc.psum_tensor(f"xacc_{layer}", [P, BANK], F32))
        with nc.Block() as plain:
            block = guarded(plain, go)

            @block.sync
            def _(sp):
                sp.sem_inc(res_free, 1)
                sp.dma_start(vals[:, :], g.values[:, 0:T * ROW]).then_inc(vals_in, 16)
                for h in range(H):
                    sp.dma_start(s1[:, h, :], g.scores[0, h].rearrange("t p -> p t")).then_inc(vals_in, 16)
                for h in range(H):
                    if h:
                        sp.wait_ge(row_used, h * T)
                    src = g.scores[1, h].rearrange("t p -> (t p)").unsqueeze(0).broadcast_to([P, N])
                    sp.dma_start(row[:, :], src).then_inc(row_in, 16)
                    with sp.Fori(0, T) as it:
                        n = it + h * T
                        sp.wait_ge(chain, n * LINKS + 1)
                        sp.dma_start(ints[:, :], adj[bass.ds(it * P, P), :]).then_inc(adj_in, 16)
                        sp.wait_ge(held, n + 1)
                        if layer < 3:
                            dst = g.sums[layer][bass.ds(it, 1), :, h * W:(h + 1) * W].rearrange("a p w -> (a p) w")
                        else:
                            dst = g.sums[layer][h, bass.ds(it * P, P), :]
                        sp.dma_start(dst, res[:, :]).then_inc(sums_out, 16)
                        sp.wait_ge(sums_out, (n + 1) * 16)
                        sp.sem_inc(res_free, 1)

            @block.vector
            def _(dve):
                dve.sem_inc(chain, LINKS)
                dve.wait_ge(vals_in, 16 * (1 + H))
                for h in range(H):
                    dve.wait_ge(row_in, 16 * (h + 1))
                    with dve.Fori(0, T) as it:
                        n = it + h * T
                        made = [0]

                        def link(ins):
                            made[0] += 1
                            ins.then_inc(chain, 1)
                            dve.wait_ge(chain, (n + 1) * LINKS + made[0])

                        dve.wait_ge(adj_in, (n + 1) * 16)
                        link(nc.vector.tensor_scalar(edge[:, :], ints[:, :], 0, None, ALU.is_gt))
                        dve.wait_ge(summed, n + 1)
                        nc.vector.tensor_scalar(e[:, :], row[:, :], s1[:, h, bass.ds(it, 1)], None,
                                                ALU.add).then_inc(row_used, 1)
                        dve.wait_ge(row_used, n + 1)
                        link(nc.vector.scalar_tensor_tensor(e[:, :], e[:, :], ALPHA, e[:, :], ALU.mult, ALU.max))
                        link(nc.vector.tensor_tensor(e[:, :], e[:, :], edge[:, :], ALU.mult))
                        link(nc.vector.tensor_scalar(edge[:, :], edge[:, :], -1.0, -NEG_INF, ALU.add, ALU.mult))
                        link(nc.vector.tensor_tensor(e[:, :], e[:, :], edge[:, :], ALU.add))
                        link(nc.vector.tensor_reduce(top[:, :], e[:, :], AX.X, ALU.max))
                        nc.vector.tensor_scalar(ntop[:, :], top[:, :], -1.0, None, ALU.mult).then_inc(shifted, 1)

            @block.scalar
            def _(act):
                with act.Fori(0, H * T) as n:
                    act.wait_ge(shifted, n + 1)
                    nc.scalar.activation(e[:, :], e[:, :], ACT.Exp, bias=ntop[:, :]).then_inc(raised, 1)
                    with act.Fori(0, GROUPS // 2) as j:
                        for b in range(2):
                            k = n * GROUPS + j * 2 + b
                            act.wait_ge(turned, k + 1)
                            act.wait_ge(added, k + 1)
                            nc.scalar.activation(pt[b][:, :], turn[b][:, :], ACT.Copy).then_inc(copied, 1)
                    act.wait_ge(summed, n + 2)
                    act.wait_ge(res_free, n + 1)
                    nc.scalar.activation(res[:, :], acc[:, 0:W], ACT.Copy).then_inc(held, 1)

            @block.tensor
            def _(pe):
                pe.sem_inc(summed, 1)
                pe.sem_inc(added, 2)
                pe.wait_ge(vals_in, 16 * (1 + H))
                with pe.Fori(0, H) as h:
                    with pe.Fori(0, T) as it:
                        n = it + h * T
                        pe.wait_ge(raised, n + 1)
                        nc.tensor.matmul(acc[:, 0:2], g.zeros[:, :], g.zeros[:, 0:2], start=True, stop=False,
                                         skip_group_check=True)
                        for j in range(GROUPS):
                            for t in range(GROUP):
                                at = (j * GROUP + t) * P
                                last = nc.tensor.transpose(turn[j % 2][:, t * P:(t + 1) * P], e[:, at:at + P],
                                                           g.identf[:, :])
                            last.then_inc(turned, 1)
                            pe.wait_ge(copied, n * GROUPS + (j + 1))
                            for t in range(GROUP):
                                rhs = vals[:, bass.ds(h * W + (j * GROUP + t) * ROW, W)]
                                last = nc.tensor.matmul(acc[:, 0:W], pt[j % 2][:, t * P:(t + 1) * P], rhs,
                                                        start=False, stop=False, skip_group_check=True)
                            last.then_inc(added, 1)
                        nc.tensor.matmul(acc[:, 0:2], g.zeros[:, :], g.zeros[:, 0:2], start=False, stop=True,
                                         skip_group_check=True).then_inc(summed, 1)


def attend(nc, sem, g, layer):
    kind = KINDS[layer]
    H, W = kind.heads, kind.width
    PH, R, J = kind.pass_heads, kind.rows, kind.step_tiles
    W3 = PIECES * W
    ROW2 = H * 2 * W3
    NB = R // P
    BLOCKS = N // R
    SUB = R // IBLK
    LT = kind.load_tiles
    STEPS_LOAD = LT // J
    LOOPS = T // (2 * LT)
    STEPS_ITER = 2 * STEPS_LOAD
    STEPS = LOOPS * STEPS_ITER
    SIGNS = 4
    WIDE = J * PH * R
    BANKC = W3 * (2 * NB * PH // 8)
    adj_in = [sem("adj_in0"), sem("adj_in1")]
    row_in = [sem("row_in0"), sem("row_in1")]
    signs, edges, masks, used = sem("signs"), sem("edges"), sem("masks"), sem("used")
    acc_ready, acc_free, sums_used, chain = sem("acc_ready"), sem("acc_free"), sem("sums_used"), sem("chain")
    stood = sem("stood")
    with ExitStack() as st:
        def sb(name, shape, dt=F32):
            return st.enter_context(nc.sbuf_tensor(f"{name}_{layer}", shape, dt))

        adj = [sb(f"adj{q}", [P, SUB, LT, IBLK], BF16) for q in range(2)]
        row = [sb(f"row{q}", [P, PH, R]) for q in range(2)]
        sgn = [sb(f"sgn{q}", [P, WIDE], BF16) for q in range(SIGNS)]
        mask = [[sb(f"mask{q}{s}", [P, WIDE], BF16) for s in range(2)] for q in range(2)]
        acc = st.enter_context(nc.psum_tensor(f"acc_{layer}", [P, 8, BANK], F32))
        raw = sb("raw", [P, 8, BANKC])
        tot = sb("tot", [P, NB * PH * 2, W])
        res = sb("res", [P, NB * PH, W])
        tmp = sb("tmp", [P, NB * PH, W])
        flag = sb("flag", [P, NB * PH])

        def accumulator(b, h, s):
            if H == 1:
                return acc[:, 2 * b + s, 0:W3]
            k = (h * 2 + s) * W3
            return acc[:, b, k:k + W3]

        with nc.Block() as block:

            @block.sync
            def _(sp):
                for ps in range(kind.passes):
                    with sp.Fori(0, BLOCKS // 2) as bb:
                        for par in range(2):
                            blk = bb * 2 + par
                            done = ps * BLOCKS
                            sp.wait_ge(signs, (blk + (done + 1)) * STEPS)
                            src = g.rows1[ps * PH:(ps + 1) * PH, bass.ds(blk * R, R)]
                            sp.dma_start(row[par][:, :, :], src.unsqueeze(0).broadcast_to([P, PH, R])).then_inc(row_in[par], 16)
                            with sp.Fori(0, LOOPS) as j:
                                for q in range(2):
                                    load = ((blk + done) * LOOPS + j) * 2 + q
                                    sp.wait_ge(edges, (load + 1) * STEPS_LOAD)
                                    tiles = bass.ds((j * 2 + q) * LT, LT)
                                    src = g.adj_t[bass.ds(blk * SUB, SUB), :, tiles, :]
                                    src = src.rearrange("s p t i -> p s t i")
                                    sp.dma_start(adj[q][:, :, :, :], src).then_inc(adj_in[q], 16)

            @block.scalar
            def _(act):
                act.sem_inc(signs, 2 * STEPS)
                act.sem_inc(acc_free, 8)
                for ps in range(kind.passes):
                    with act.Fori(0, BLOCKS // 2) as bb:
                        for par in range(2):
                            blk = bb * 2 + par + ps * BLOCKS
                            act.wait_ge(row_in[par], (bb + (ps * (BLOCKS // 2) + 1)) * 16)
                            with act.Fori(0, LOOPS) as j:
                                for k in range(STEPS_ITER):
                                    n = (blk * LOOPS + j) * STEPS_ITER + k
                                    act.wait_ge(masks, n + 1)
                                    for u in range(J * PH):
                                        jt, h = (u, 0) if H == 1 else (0, u)
                                        col = ((j * STEPS_ITER + k) * J + jt) * H + (ps * PH + h)
                                        last = nc.scalar.activation(sgn[k % SIGNS][:, u * R:(u + 1) * R], row[par][:, h, :],
                                                                    ACT.Sign, bias=g.score[:, bass.ds(col, 1)])
                                    last.then_inc(signs, 1)
                            act.wait_ge(sums_used, blk + 1)
                            for b in range(8):
                                act.wait_ge(acc_ready, blk * 8 + (b + 1))
                                nc.scalar.activation(raw[:, b, :], acc[:, b, 0:BANKC], ACT.Copy).then_inc(acc_free, 1)

            @block.vector
            def _(dve):
                dve.sem_inc(edges, 2 * STEPS_LOAD)
                dve.sem_inc(masks, SIGNS)
                with dve.Fori(0, kind.passes * BLOCKS * LOOPS) as it:
                    def parts(k):
                        n = it * STEPS_ITER + k
                        dve.wait_ge(used, n + 1)
                        dve.wait_ge(edges, n + (1 + 2 * STEPS_LOAD))
                        nc.vector.tensor_scalar(mask[k % 2][0][:, :], sgn[k % SIGNS][:, :], 0.0, None, ALU.max)
                        nc.vector.tensor_scalar(mask[k % 2][1][:, :], sgn[k % SIGNS][:, :], -1.0, 0.0,
                                                ALU.mult, ALU.max).then_inc(masks, 1)

                    for k in range(STEPS_ITER):
                        n = it * STEPS_ITER + k
                        q, kk = k // STEPS_LOAD, k % STEPS_LOAD
                        if kk == 0:
                            dve.wait_ge(adj_in[q], (it + 1) * 16)
                        dve.wait_ge(signs, n + (1 + 2 * STEPS))
                        if H == 1:
                            s = sgn[k % SIGNS][:, :]
                            a = adj[q][:, 0, kk * J:(kk + 1) * J, :].rearrange("p t i -> p (t i)")
                        else:
                            s = sgn[k % SIGNS][:, :].rearrange("p (h s i) -> p h s i", h=PH, s=SUB)
                            a = adj[q][:, :, kk, :].unsqueeze(1).broadcast_to([P, PH, SUB, IBLK])
                        nc.vector.tensor_tensor(s, s, a, ALU.mult).then_inc(edges, 1)
                        if k:
                            parts(k - 1)
                    parts(STEPS_ITER - 1)

            @block.tensor
            def _(pe):
                pe.sem_inc(used, 2)
                for ps in range(kind.passes):
                    with pe.Fori(0, BLOCKS) as bb:
                        blk = bb + ps * BLOCKS
                        for b in range(8):
                            pe.wait_ge(acc_free, blk * 8 + (b + 1))
                            nc.tensor.matmul(acc[:, b, 0:2], g.zeros[:, :], g.zeros[:, 0:2], start=True, stop=False,
                                             skip_group_check=True)
                        with pe.Fori(0, LOOPS) as j:
                            for k in range(STEPS_ITER):
                                n = (blk * LOOPS + j) * STEPS_ITER + k
                                pe.wait_ge(masks, n + (1 + SIGNS))
                                for jt in range(J):
                                    tile = (j * STEPS_ITER + k) * J + jt
                                    for b in range(NB):
                                        for h in range(PH):
                                            for s in range(2):
                                                at = (jt if H == 1 else h) * R + b * P
                                                rhs = g.split[:, bass.ds(tile * ROW2 + ((ps * PH + h) * 2 + s) * W3, W3)]
                                                last = nc.tensor.matmul(accumulator(b, h, s),
                                                                        mask[k % 2][s][:, at:at + P], rhs,
                                                                        start=False, stop=False, skip_group_check=True)
                                last.then_inc(used, 1)
                        for b in range(8):
                            nc.tensor.matmul(acc[:, b, 0:2], g.zeros[:, :], g.zeros[:, 0:2], start=False, stop=True,
                                             skip_group_check=True).then_inc(acc_ready, 1)

            @block.gpsimd
            def _(pool):
                pool.sem_inc(sums_used, 1)
                LINKS = 7
                each = 16 if layer < 3 else 16 * PH
                before = g.pool_stores
                g.pool_stores += each * kind.passes * BLOCKS
                for ps in range(kind.passes):
                    with pool.Fori(0, BLOCKS) as bb:
                        blk = bb + ps * BLOCKS
                        made = [0]

                        def link(ins):
                            made[0] += 1
                            ins.then_inc(chain, 1)
                            pool.wait_ge(chain, blk * LINKS + made[0])

                        pool.wait_ge(acc_free, blk * 8 + 16)
                        r = raw[:, :, :].rearrange("p b (c w) -> p (b c) w", w=W3)
                        link(nc.gpsimd.tensor_tensor(tot[:, :, :], r[:, :, 0:W], r[:, :, W:2 * W], ALU.add))
                        nc.gpsimd.tensor_tensor(tot[:, :, :], tot[:, :, :], r[:, :, 2 * W:3 * W], ALU.add).then_inc(sums_used, 1)
                        pool.wait_ge(sums_used, blk + 2)
                        two = tot[:, :, :].rearrange("p (u s) w -> p u s w", s=2)

                        def factor(v):
                            if H == 1:
                                v = v[:, bass.ds(bb * NB, NB)].unsqueeze(2)
                                return v.broadcast_to([P, NB, W])
                            v = v[:, bass.ds(bb * (NB * H), NB * H)].rearrange("p (b h) -> p b h", h=H)
                            return v[:, :, ps * PH:(ps + 1) * PH].unsqueeze(3).broadcast_to([P, NB, PH, W])

                        def shaped(v):
                            return v if H == 1 else v.rearrange("p (b h) w -> p b h w", h=PH)

                        link(nc.gpsimd.tensor_tensor(shaped(res[:, :, :]), shaped(two[:, :, 0, :]), factor(g.ra), ALU.mult))
                        link(nc.gpsimd.tensor_tensor(shaped(tmp[:, :, :]), shaped(two[:, :, 1, :]), factor(g.rb), ALU.mult))
                        link(nc.gpsimd.tensor_tensor(res[:, :, :], res[:, :, :], tmp[:, :, :], ALU.add))
                        pool.sem_inc(stood, 1)
                        link(nc.gpsimd.tensor_scalar(flag[:, :], res[:, :, W - 1], 0.0, None, ALU.is_equal))
                        cs = g.colsum[:, ps * PH * W:(ps + 1) * PH * W]
                        if H == 1:
                            cs = cs.unsqueeze(1).broadcast_to([P, NB, W])
                            fl = flag[:, :].unsqueeze(2).broadcast_to([P, NB, W])
                        else:
                            cs = cs.rearrange("p (h w) -> p h w", h=PH).unsqueeze(1).broadcast_to([P, NB, PH, W])
                            fl = flag[:, :].rearrange("p (b h) -> p b h", h=PH).unsqueeze(3).broadcast_to([P, NB, PH, W])
                        link(nc.gpsimd.tensor_tensor(shaped(tmp[:, :, :]), fl, cs, ALU.mult))
                        link(nc.gpsimd.tensor_tensor(res[:, :, :], res[:, :, :], tmp[:, :, :], ALU.add))
                        if layer < 3:
                            dst = g.sums[layer][bass.ds(bb * NB, NB), :, ps * PH * W:(ps + 1) * PH * W]
                            pool.dma_start(dst.rearrange("b p w -> p b w"),
                                           res[:, :, :].rearrange("p (b h) w -> p b (h w)", h=PH)).then_inc(g.pool_stored, 16)
                        else:
                            for h in range(PH):
                                dst = g.sums[layer][ps * PH + h, bass.ds(bb * R, R), :]
                                pool.dma_start(dst.rearrange("(b p) w -> p b w", p=P),
                                               res[:, :, :].rearrange("p (b h) w -> p b h w", h=PH)[:, :, h, :]
                                               ).then_inc(g.pool_stored, 16)
                        pool.wait_ge(g.pool_stored, (blk + 1) * each + before)
                        pool.sem_inc(stood, 1)


def gat_kernel(nc, x, adj, L0_W, L0_a1, L0_a2, L1_W, L1_a, L2_W, L2_a, L3_W, L3_a, out):
    D = F // 4
    one = lambda v: v.rearrange("(h d) -> h d", h=1)
    weights = [
        (L0_W, one(L0_a1), one(L0_a2)),
        (L1_W, L1_a[0, :, 0:D], L1_a[0, :, D:2 * D]),
        (L2_W, L2_a[0:F, :].rearrange("d h -> h d"), L2_a[F:2 * F, :].rearrange("d h -> h d")),
        (L3_W, L3_a[:, D:2 * D, 0], L3_a[:, 0:D, 0]),
    ]
    with ExitStack() as ctx:
        ctx.enter_context(nc.allow_non_contiguous_dma("weights"))
        g = tensors(nc, ctx)
        with stage_semaphores(nc, "setup") as sem:
            setup(nc, sem, g, weights)
        with ExitStack() as factored:
            g.split = factored.enter_context(nc.sbuf_tensor("split", [P, T * STAT_MAX], BF16))
            with stage_semaphores(nc, "turn") as sem:
                transpose_adjacency(nc, sem, g, adj)
            for layer in range(4):
                with stage_semaphores(nc, f"nodes{layer}") as sem:
                    update_nodes(nc, sem, g, layer, x, out)
                with stage_semaphores(nc, f"attend{layer}") as sem:
                    attend(nc, sem, g, layer)
            with stage_semaphores(nc, "nodes4") as sem:
                update_nodes(nc, sem, g, 4, x, out)
        with stage_semaphores(nc, "decide") as sem:
            decide(nc, sem, g)
        go = nc.values_load(g.exact[0:1, 0:1], min_val=0, max_val=1)
        for layer in range(4):
            with stage_semaphores(nc, f"xnodes{layer}") as sem:
                update_nodes(nc, sem, g, layer, x, out, go)
            with stage_semaphores(nc, f"xattend{layer}") as sem:
                attend_exact(nc, sem, g, layer, adj, go)
        with stage_semaphores(nc, "xnodes4") as sem:
            update_nodes(nc, sem, g, 4, x, out, go)


_INS = ["x", "adj", "L0_gnn_W", "L0_gnn_a1", "L0_gnn_a2", "L1_gnn_W", "L1_gnn_a", "L2_gnn_W", "L2_gnn_a",
        "L3_gnn_W", "L3_gnn_a"]


def kernel(**inputs):
    import numpy as _np
    import concourse.bacc as _bacc
    from concourse import mybir as _mybir
    from concourse.bass_utils import run_bass_kernel_spmd as _run

    nc = _bacc.Bacc("TRN2", target_bir_lowering=False, num_devices=1)
    arrays, args = {}, []
    for name in _INS:
        a = _np.ascontiguousarray(inputs[name])
        arrays[f"in_{name}"] = a
        args.append(nc.dram_tensor(f"in_{name}", a.shape, _mybir.dt.from_np(a.dtype), kind="ExternalInput").ap())
    args.append(nc.dram_tensor("out_nodes", (N, F), F32, kind="ExternalOutput").ap())
    gat_kernel(nc, *args)
    r = _run(nc, [arrays], core_ids=[0])
    return r.results[0]["out_nodes"]
```

```python
import math
from contextlib import ExitStack, contextmanager

import concourse.bass as bass
from concourse import mybir

F32 = mybir.dt.float32
BF16 = mybir.dt.bfloat16
I32 = mybir.dt.int32
ALU = mybir.AluOpType
ACT = mybir.ActivationFunctionType
AX = mybir.AxisListType
RMAX = bass.bass_isa.ReduceOp.max

P = 128
N = 8192
F = 128
T = N // P
ALPHA = 0.2
EPS = 1e-5
BANK = 512
PIECES = 3
IBLK = 512
NEG_INF = -9000000000000000.0
WIDEST = 60.0
TINY = 2.0 ** -60


class Kind:

    def __init__(self, heads):
        self.heads, self.width = heads, F // heads + 1


class Guarded:

    def __init__(self, sync, scalar, vector, tensor, gpsimd):
        self.sync, self.scalar, self.vector, self.tensor, self.gpsimd = sync, scalar, vector, tensor, gpsimd


class Shared:
    pass


KINDS = [Kind(1), Kind(4), Kind(1), Kind(4)]
ROW_MAX = max(k.heads * k.width for k in KINDS)
STAT_MAX = max(2 * k.heads * PIECES * k.width for k in KINDS)
AUG = F + 2 * 4


def guarded(block, go):
    if go is None:
        return block

    def only_if(attach):
        def take(program):
            def body(engine):
                with engine.If(go > 0):
                    program(engine)
                with engine.Else():
                    engine.nop()

            attach(body)

        return take

    return Guarded(sync=only_if(block.sync), scalar=only_if(block.scalar), vector=only_if(block.vector),
                           tensor=only_if(block.tensor), gpsimd=only_if(block.gpsimd))


@contextmanager
def stage_semaphores(nc, tag):
    with ExitStack() as st:
        made = []

        def sem(name):
            made.append(st.enter_context(nc.semaphore(f"{tag}_{name}")))
            return made[-1]

        yield sem
        with nc.Block() as block:

            @block.gpsimd
            def _(pool):
                for s in made:
                    pool.sem_clear(s)


def tensors(nc, ctx):
    def sb(name, shape, dt):
        return ctx.enter_context(nc.sbuf_tensor(name, shape, dt))

    g = Shared()
    g.identf = sb("identf", [P, P], F32)
    g.identb = sb("identb", [P, P], BF16)
    g.zeros = sb("zeros", [P, P], BF16)
    g.onesf = sb("onesf", [P, P], F32)
    g.waug = sb("waug", [P, 4, AUG], F32)
    g.widest = sb("widest", [P, 1], F32)
    g.exact = sb("exact", [P, 1], I32)
    g.score = sb("score", [P, T * 4], F32)
    g.ra = sb("ra", [P, T * 4], F32)
    g.rb = sb("rb", [P, T * 4], F32)
    g.colsum = sb("colsum", [P, ROW_MAX], F32)
    g.adj_t = nc.dram_tensor("adj_t", [N // IBLK, P, T, IBLK], BF16, kind="Internal").ap()
    g.scores = nc.dram_tensor("scores", [2, 4, T, P], F32, kind="Internal").ap()
    g.values = nc.dram_tensor("values", [P, T * ROW_MAX], F32, kind="Internal").ap()
    g.nodes = nc.dram_tensor("nodes", [N, F], F32, kind="Internal").ap()
    g.rows1 = nc.dram_tensor("rows1", [4, N], F32, kind="Internal").ap()
    g.sums = [nc.dram_tensor(f"sums{l}", [T, P, k.heads * k.width] if l < 3 else [k.heads, N, k.width], F32,
                             kind="Internal").ap() for l, k in enumerate(KINDS)]
    g.pool_stored = ctx.enter_context(nc.semaphore("pool_stored"))
    g.pool_stores = 0
    return g


def setup(nc, sem, g, weights):
    blank, weights_in, made, summed = sem("blank"), sem("weights_in"), sem("made"), sem("summed")
    with ExitStack() as st:
        vecs = st.enter_context(nc.sbuf_tensor("vecs", [P, 4, 2, F], F32))
        prod = st.enter_context(nc.sbuf_tensor("prod", [P, 4, 2, F], F32))
        with nc.Block() as block:

            @block.sync
            def _(sp):
                for l, (w, score_i, score_j) in enumerate(weights):
                    if len(w.shape) == 3:
                        dst = g.waug[:, l, 0:F].rearrange("p (h d) -> p h d", h=w.shape[0])
                        sp.dma_start(dst, w.rearrange("h p d -> p h d")).then_inc(weights_in, 16)
                    else:
                        sp.dma_start(g.waug[:, l, 0:F], w).then_inc(weights_in, 16)
                    for k, a in enumerate((score_i, score_j)):
                        h, d = a.shape
                        dst = vecs[:, l, k, :].rearrange("p (h d) -> p h d", h=h)
                        sp.dma_start(dst, a.unsqueeze(0).broadcast_to([P, h, d])).then_inc(weights_in, 16)

            @block.gpsimd
            def _(pool):
                nc.gpsimd.memset(g.identf[:, :], 0.0).then_inc(blank, 1)
                nc.gpsimd.memset(g.identb[:, :], 0.0).then_inc(blank, 1)
                nc.gpsimd.memset(g.zeros[:, :], 0.0).then_inc(blank, 1)
                nc.gpsimd.memset(g.onesf[:, :], 1.0).then_inc(blank, 1)
                nc.gpsimd.memset(g.widest[:, :], 0.0)
                pool.wait_ge(blank, 4)
                for m in (g.identf, g.identb):
                    nc.gpsimd.affine_select(out=m[:, :], in_=m[:, :], compare_op=ALU.not_equal, fill=1.0,
                                            base=0, pattern=[[-1, P]], channel_multiplier=1).then_inc(blank, 1)

            @block.vector
            def _(dve):
                dve.wait_ge(weights_in, 16 * 12)
                for l in range(4):
                    nc.vector.tensor_tensor(prod[:, l], vecs[:, l],
                                            g.waug[:, l, 0:F].unsqueeze(1).broadcast_to([P, 2, F]),
                                            ALU.mult).then_inc(made, 1)
                dve.wait_ge(made, 4)
                for l, k in enumerate(KINDS):
                    dst = g.waug[:, l, F:F + 2 * k.heads].rearrange("p (k h) -> p k h", k=2)
                    src = prod[:, l].rearrange("p k (h d) -> p k h d", h=k.heads)
                    nc.vector.tensor_reduce(dst, src, AX.X, ALU.add).then_inc(summed, 1)


def transpose_adjacency(nc, sem, g, adj):
    COLS = 1024
    NT, NI = COLS // P, IBLK // P
    ITEMS = N // COLS
    int_in, int_used, ones_ready = [sem("int_in0"), sem("int_in1")], sem("int_used"), sem("ones_ready")
    turned, bank_free, packed = sem("turned"), sem("bank_free"), sem("packed")
    stored, out_free = [sem("stored0"), sem("stored1")], sem("out_free")
    with ExitStack() as st:
        raw = [st.enter_context(nc.sbuf_tensor(f"raw{b}", [P, NI, COLS], I32)) for b in range(2)]
        ones = [st.enter_context(nc.sbuf_tensor(f"ones{b}", [P, NI, COLS], BF16)) for b in range(2)]
        pack = [st.enter_context(nc.sbuf_tensor(f"pack{b}", [P, NT, IBLK], BF16)) for b in range(2)]
        turn = st.enter_context(nc.psum_tensor("turn", [P, 8, 2, IBLK], BF16))
        BANKS = NT // 2
        with nc.Block() as block:

            @block.sync
            def _(sp):
                with sp.Fori(0, N // IBLK) as ib:
                    with sp.Fori(0, ITEMS // 2) as jj:
                        for b in range(2):
                            n = (ib * (ITEMS // 2) + jj) * 2 + b
                            sp.wait_ge(int_used, n + 1)
                            src = adj[bass.ds(ib * IBLK, IBLK), bass.ds((jj * 2 + b) * COLS, COLS)]
                            sp.dma_start(raw[b][:, :, :], src.rearrange("(t p) c -> p t c", p=P)).then_inc(int_in[b], 16)

            @block.vector
            def _(dve):
                dve.sem_inc(int_used, 2)
                with dve.Fori(0, N // IBLK * ITEMS // 2) as jj:
                    for b in range(2):
                        n = jj * 2 + b
                        dve.wait_ge(int_in[b], (jj + 1) * 16)
                        dve.wait_ge(turned, n + 1)
                        nc.vector.tensor_scalar(ones[b][:, :, :], raw[b][:, :, :], 0, None,
                                                ALU.is_gt).then_inc(int_used, 1)

            @block.tensor
            def _(pe):
                pe.sem_inc(turned, 2)
                with pe.Fori(0, N // IBLK * ITEMS // 2) as jj:
                    for b in range(2):
                        n = jj * 2 + b
                        pe.wait_ge(int_used, n + 3)
                        for k in range(BANKS):
                            pe.wait_ge(bank_free, (n * BANKS + k) + 1)
                            for t in range(2 * k, 2 * k + 2):
                                for i in range(NI):
                                    last = nc.tensor.transpose(turn[:, b * BANKS + k, t % 2, i * P:(i + 1) * P],
                                                               ones[b][:, i, t * P:(t + 1) * P], g.identb[:, :])
                            if k < BANKS - 1:
                                last.then_inc(packed, 1)
                        last.then_inc(turned, 1)

            @block.scalar
            def _(act):
                act.sem_inc(bank_free, 8)
                with act.Fori(0, N // IBLK) as ib:
                    with act.Fori(0, ITEMS // 2) as jj:
                        for b in range(2):
                            n = (ib * (ITEMS // 2) + jj) * 2 + b
                            act.wait_ge(out_free, n + 1)
                            for k in range(BANKS):
                                if k < BANKS - 1:
                                    act.wait_ge(packed, n * (BANKS - 1) + k + 1)
                                else:
                                    act.wait_ge(turned, n + 3)
                                last = nc.scalar.activation(pack[b][:, 2 * k:2 * k + 2, :], turn[:, b * BANKS + k],
                                                            ACT.Copy, scale=-1.0)
                                last.then_inc(bank_free, 1)
                            act.wait_ge(bank_free, (n + 1) * BANKS + 8)
                            dst = g.adj_t[bass.ds(ib, 1), :, bass.ds((jj * 2 + b) * NT, NT), :]
                            act.dma_start(dst.rearrange("b p t i -> (b p) t i"), pack[b][:, :, :]).then_inc(stored[b], 16)

            @block.gpsimd
            def _(pool):
                pool.sem_inc(out_free, 2)
                with pool.Fori(0, N // IBLK * ITEMS // 2) as jj:
                    for b in range(2):
                        pool.wait_ge(stored[b], (jj + 1) * 16)
                        pool.sem_inc(out_free, 1)


def update_nodes(nc, sem, g, layer, x_in, out, go=None):
    before = KINDS[layer - 1] if layer else None
    kind = KINDS[layer] if layer < 4 else None
    elu = layer < 4
    tag = f"{layer}" if go is None else f"{layer}x"
    PART = 8
    PARTS = T // PART
    with ExitStack() as st:
        def sb(name, shape, dt=F32):
            return st.enter_context(nc.sbuf_tensor(f"{name}_{tag}", shape, dt))

        x = sb("x", [P, T, F])
        vals = sb("vals", [P, T * ROW_MAX])
        stats = sb("stats", [P, PART, 6])
        pair = sb("pair", [P, PART, 2])
        mv = sb("mv", [P, T, 2])
        rstd = sb("rstd", [P, T])
        x_landed, s_landed = sem("x_landed"), sem("s_landed")
        chain, low, raised, x_ready, measured = sem("chain"), sem("low"), sem("raised"), sem("x_ready"), sem("measured")
        stood = sem("stood")
        x_src = x_in if layer < 2 else g.nodes
        with ExitStack() as st1:
            frac = st1.enter_context(nc.sbuf_tensor(f"frac_{tag}", [P, PART, F], F32))
            expm = st1.enter_context(nc.sbuf_tensor(f"expm_{tag}", [P, PART * F], F32))
            rden = st1.enter_context(nc.sbuf_tensor(f"rden_{tag}", [P, PART * 4], F32))
            with nc.Block() as plain:
                block = guarded(plain, go)

                @block.sync
                def _(sp):
                    HALVES = PARTS // 4 if layer == 4 else PARTS
                    with sp.Fori(0, PARTS // HALVES) as head:
                        with sp.Fori(0, HALVES) as half:
                            p = head * HALVES + half
                            rows = x_src[bass.ds(p * (PART * P), PART * P), :].rearrange("(t p) f -> p t f", p=P)
                            sp.dma_start(x[:, bass.ds(p * PART, PART), :], rows).then_inc(x_landed, 16)
                            if before:
                                row = before.heads * before.width
                                if layer < 4:
                                    src = g.sums[layer - 1][bass.ds(p * PART, PART)].rearrange("t p w -> p t w")
                                else:
                                    src = g.sums[3][bass.ds(head, 1), bass.ds(half * (PART * P * 4), PART * P * 4), :]
                                    src = src.rearrange("a (t p i) w -> p (a t) (i w)", p=P, i=4)
                                dst = vals[:, bass.ds(p * (PART * row), PART * row)]
                                sp.dma_start(dst.rearrange("p (t w) -> p t w", t=PART), src).then_inc(s_landed, 16)
                                sp.wait_ge(s_landed, (p + 1) * 16)
                            sp.wait_ge(x_landed, (p + 1) * 16)
                            sp.sem_inc(stood, 1)

                @block.gpsimd
                def _(pool):
                    if before:
                        dst = out if layer == 4 else g.nodes
                        with pool.Fori(0, PARTS) as p:
                            pool.wait_ge(x_ready, p + 1)
                            rows = dst[bass.ds(p * (PART * P), PART * P), :].rearrange("(t p) f -> p t f", p=P)
                            pool.dma_start(rows, x[:, bass.ds(p * PART, PART), :]).then_inc(g.pool_stored, 16)
                        g.pool_stores += 16 * PARTS
                        pool.wait_ge(g.pool_stored, g.pool_stores)

                @block.scalar
                def _(act):
                    if before and elu:
                        with act.Fori(0, PARTS) as p:
                            act.wait_ge(low, p + 1)
                            nc.scalar.activation(expm[:, :], expm[:, :], ACT.Exp).then_inc(raised, 1)

                @block.vector
                def _(dve):
                    LINKS = (3 if elu else 2) if before else 0
                    with dve.Fori(0, PARTS) as p:
                        made = [0]

                        def link(ins):
                            made[0] += 1
                            ins.then_inc(chain, 1)
                            dve.wait_ge(chain, p * LINKS + made[0])

                        xp = x[:, bass.ds(p * PART, PART), :]
                        dve.wait_ge(x_landed, (p + 1) * 16)
                        if before:
                            H, W = before.heads, before.width
                            s = vals[:, bass.ds(p * (PART * H * W), PART * H * W)]
                            s = s.rearrange("p (u w) -> p u w", w=W)
                            dve.wait_ge(s_landed, (p + 1) * 16)
                            link(nc.vector.reciprocal(rden[:, 0:PART * H], s[:, :, W - 1]))
                            f = frac[:, :, :].rearrange("p t (h d) -> p (t h) d", h=H)
                            link(nc.vector.tensor_tensor(
                                f, s[:, :, 0:W - 1],
                                rden[:, 0:PART * H].unsqueeze(2).broadcast_to([P, PART * H, W - 1]), ALU.mult))
                            flat = frac[:, :, :].rearrange("p t f -> p (t f)")
                            if elu:
                                nc.vector.tensor_scalar(expm[:, :], flat, 0.0, None, ALU.min).then_inc(low, 1)
                                dve.wait_ge(raised, p + 1)
                                link(nc.vector.scalar_tensor_tensor(expm[:, :], flat, 0.0, expm[:, :],
                                                                    ALU.max, ALU.add))
                                nc.vector.scalar_tensor_tensor(xp, expm[:, :].rearrange("p (t f) -> p t f", f=F), -1.0,
                                                               xp, ALU.add, ALU.add).then_inc(x_ready, 1)
                            else:
                                nc.vector.tensor_tensor(xp, frac[:, :, :], xp, ALU.add).then_inc(x_ready, 1)
                            dve.wait_ge(x_ready, p + 1)
                        if kind:
                            dve.sem_inc(stood, 1)
                            for t in range(PART):
                                last = nc.vector.bn_stats(stats[:, t, :], x[:, bass.ds(p * PART + t, 1), :]
                                                          .rearrange("p a f -> p (a f)"))
                            last.then_inc(measured, 1)
                            dve.wait_ge(measured, 3 * p + 1)
                            dve.sem_inc(stood, 1)
                            for t in range(PART):
                                last = nc.vector.bn_aggr(pair[:, t, :], stats[:, t, :])
                            last.then_inc(measured, 1)
                            dve.wait_ge(measured, 3 * p + 2)
                            nc.vector.tensor_copy(mv[:, bass.ds(p * PART, PART), :], pair[:, :, :]).then_inc(measured, 1)
                            dve.wait_ge(measured, 3 * p + 3)
        if not kind:
            return
        H, W = kind.heads, kind.width
        ROW = H * W
        CH = 4
        CHUNKS = T // CH
        cols = F + 2 * H
        scol = sb("scol", [P, T, 2 * H])
        with ExitStack() as st2:
            hn = [st2.enter_context(nc.sbuf_tensor(f"hn{b}_{tag}", [P, CH, F], F32)) for b in range(2)]
            ht = [st2.enter_context(nc.sbuf_tensor(f"ht{b}_{tag}", [P, CH * P], F32)) for b in range(2)]
            srow = [st2.enter_context(nc.sbuf_tensor(f"srow{b}_{tag}", [H, CH * P], F32)) for b in range(2)]
            pt = [st2.enter_context(nc.psum_tensor(f"pt{b}_{tag}", [P, CH * P], F32)) for b in range(2)]
            pv = [st2.enter_context(nc.psum_tensor(f"pv{b}_{tag}", [P, 2, BANK], F32)) for b in range(2)]
            ps = [st2.enter_context(nc.psum_tensor(f"ps{b}_{tag}", [P, BANK], F32)) for b in range(2)]
            rooted, inverse = sem("rooted"), sem("inverse")
            h_ready, turned, ht_ready, projected = sem("h_ready"), sem("turned"), sem("ht_ready"), sem("projected")
            v_copied, row_made, row_ready = sem("v_copied"), sem("row_made"), sem("row_ready")
            row_out, row_free, ones_set = sem("row_out"), sem("row_free"), sem("ones_set")
            with nc.Block() as plain:
                block = guarded(plain, go)

                @block.gpsimd
                def _(pool):
                    u = vals[:, 0:T * ROW].rearrange("p (u w) -> p u w", w=W)
                    nc.gpsimd.memset(u[:, :, W - 1], 1.0).then_inc(ones_set, 1)

                @block.sync
                def _(sp):
                    sp.sem_inc(row_free, 2)
                    with sp.Fori(0, CHUNKS // 2) as cc:
                        for b in range(2):
                            c = cc * 2 + b
                            sp.wait_ge(row_ready, c + 1)
                            sp.dma_start(g.rows1[0:H, bass.ds(c * (CH * P), CH * P)], srow[b][:, :]).then_inc(row_out, 16)
                            sp.wait_ge(row_out, (c + 1) * 16)
                            sp.sem_inc(row_free, 1)

                @block.vector
                def _(dve):
                    nc.vector.tensor_scalar(rstd[:, :], mv[:, :, 1], EPS, None, ALU.add).then_inc(rooted, 1)
                    dve.wait_ge(rooted, 2)
                    nc.vector.reciprocal(rstd[:, :], rstd[:, :]).then_inc(inverse, 1)
                    dve.wait_ge(inverse, 1)
                    dve.sem_inc(row_made, 2)
                    with dve.Fori(0, CHUNKS // 2) as cc:
                        for b in range(2):
                            c = cc * 2 + b
                            dve.wait_ge(turned, c + 1)
                            for t in range(CH):
                                tile = bass.ds(c * CH + t, 1)
                                last = nc.vector.tensor_scalar(
                                    hn[b][:, t, :], x[:, tile, :].rearrange("p a f -> p (a f)"),
                                    mv[:, tile, 0:1].rearrange("p a f -> p (a f)"), rstd[:, tile],
                                    ALU.subtract, ALU.mult)
                            last.then_inc(h_ready, 1)
                            dve.wait_ge(projected, c + 1)
                            dve.wait_ge(row_free, c + 1)
                            nc.vector.tensor_scalar(srow[b][:, :], ps[b][0:H, :], TINY, None, ALU.add).then_inc(row_made, 1)
                            dve.wait_ge(row_made, c + 3)
                            bits = srow[b][:, :].bitcast(I32)
                            nc.vector.tensor_scalar(bits, bits, 1, None, ALU.bitwise_or).then_inc(row_ready, 1)

                @block.tensor
                def _(pe):
                    pe.sem_inc(turned, 2)
                    with pe.Fori(0, CHUNKS // 2) as cc:
                        for b in range(2):
                            c = cc * 2 + b
                            pe.wait_ge(h_ready, c + 1)
                            pe.wait_ge(ht_ready, c + 1)
                            for t in range(CH):
                                last = nc.tensor.transpose(pt[b][:, t * P:(t + 1) * P], hn[b][:, t, :], g.identf[:, :])
                            last.then_inc(turned, 1)
                            pe.wait_ge(ht_ready, c + 3)
                            pe.wait_ge(v_copied, c + 1)
                            pe.wait_ge(row_made, c + 1)
                            for t in range(CH):
                                nc.tensor.matmul(pv[b][:, t // 2, (t % 2) * cols:(t % 2 + 1) * cols],
                                                 ht[b][:, t * P:(t + 1) * P], g.waug[:, layer, 0:cols],
                                                 start=True, stop=True)
                            nc.tensor.matmul(ps[b][0:H, :], g.waug[:, layer, F:F + H], ht[b][:, :],
                                             start=True, stop=True).then_inc(projected, 1)

                @block.scalar
                def _(act):
                    act.wait_ge(rooted, 1)
                    nc.scalar.activation(rstd[:, :], rstd[:, :], ACT.Sqrt).then_inc(rooted, 1)
                    act.sem_inc(ht_ready, 2)
                    act.sem_inc(v_copied, 2)
                    with act.Fori(0, CHUNKS // 2) as cc:
                        for b in range(2):
                            c = cc * 2 + b
                            act.wait_ge(turned, c + 3)
                            nc.scalar.activation(ht[b][:, :], pt[b][:, :], ACT.Relu).then_inc(ht_ready, 1)
                            act.wait_ge(projected, c + 1)
                            for k in range(2):
                                src = pv[b][:, k, 0:2 * cols].rearrange("p (t c) -> p t c", c=cols)[:, :, F:cols]
                                nc.scalar.activation(scol[:, bass.ds(c * CH + 2 * k, 2), :], src, ACT.Copy)
                                dst = vals[:, bass.ds((c * CH + 2 * k) * ROW, 2 * ROW)]
                                dst = dst.rearrange("p (t h w) -> p t h w", t=2, h=H)[:, :, :, 0:W - 1]
                                src = pv[b][:, k, 0:2 * cols].rearrange("p (t c) -> p t c", c=cols)[:, :, 0:F]
                                src = src.rearrange("p t (h d) -> p t h d", h=H)
                                last = nc.scalar.activation(dst, src, ACT.Copy)
                            last.then_inc(v_copied, 1)

        if go is not None:
            store_for_exact(nc, sem, g, kind, scol, vals, go)
            return

        with ExitStack() as st3:
            def sb3(name, shape, dt=F32):
                return st3.enter_context(nc.sbuf_tensor(f"{name}_{tag}", shape, dt))

            ends, most = sb3("ends", [P, 2 * H]), sb3("most", [P, 2 * H])
            tlow, thigh, u = sb3("tlow", [P, T, H]), sb3("thigh", [P, T, H]), sb3("u", [P, T, H])
            col = [sb3("ca", [P, T, H]), sb3("cb", [P, T, H])]
            UT = 4
            whole = [sb3(f"whole{b}", [P, UT * ROW]) for b in range(2)]
            rest = [sb3(f"rest{b}", [P, UT * ROW]) for b in range(2)]
            ptot = st3.enter_context(nc.psum_tensor(f"ptot_{tag}", [P, BANK], F32))
            UNITS = T // UT * 2
            ends_ready, most_ready, spread, exps = sem("ends_ready"), sem("most_ready"), sem("spread"), sem("exps")
            totalled, ranged = sem("totalled"), sem("ranged")
            wholes, highs, rests, mids, lows = sem("wholes"), sem("highs"), sem("rests"), sem("mids"), sem("lows")
            pieces = g.split[:, 0:T * 2 * PIECES * ROW].rearrange("p (t c q w) -> p t c q w", t=T, q=PIECES, w=W)

            def piece(cc, side, q):
                v = pieces[:, bass.ds(cc * UT, UT), :, q, :]
                if H == 1:
                    return v[:, :, side:side + 1, :]
                v = v.rearrange("p t (g c) w -> p (t g) c w", c=4)
                return v[:, :, 1:3, :] if side == 0 else v[:, :, 0:4:3, :]

            def unit(buf):
                return buf[:, :].rearrange("p (t h w) -> p t h w", h=min(H, 2), w=W)

            with nc.Block() as plain:
                block = guarded(plain, go)

                @block.gpsimd
                def _(pool):
                    pool.wait_ge(ends_ready, 2)
                    nc.gpsimd.partition_all_reduce(most[:, :], ends[:, :], P, RMAX).then_inc(most_ready, 1)
                    pool.wait_ge(exps, 2)
                    with pool.Fori(0, T // UT) as cc:
                        for side in range(2):
                            pool.wait_ge(rests, cc * 2 + side + 1)
                            v = vals[:, bass.ds(cc * (UT * ROW), UT * ROW)].rearrange("p (t h w) -> p t h w", t=UT, h=H)
                            c = col[side][:, bass.ds(cc * UT, UT), :].unsqueeze(3).broadcast_to([P, UT, H, W])
                            dst = whole[side][:, :].rearrange("p (t h w) -> p t h w", t=UT, h=H)
                            nc.gpsimd.tensor_tensor(dst, v, c, ALU.mult).then_inc(wholes, 1)

                @block.tensor
                def _(pe):
                    nc.tensor.matmul(ptot[:, 0:ROW], g.onesf[:, :], vals[:, 0:ROW], start=True, stop=False)
                    with pe.Fori(1, T - 1) as t:
                        nc.tensor.matmul(ptot[:, 0:ROW], g.onesf[:, :], vals[:, bass.ds(t * ROW, ROW)],
                                         start=False, stop=False)
                    nc.tensor.matmul(ptot[:, 0:ROW], g.onesf[:, :], vals[:, (T - 1) * ROW:T * ROW],
                                     start=False, stop=True).then_inc(totalled, 1)

                @block.scalar
                def _(act):
                    act.wait_ge(spread, 2)
                    nc.scalar.activation(col[0][:, :, :], u[:, :, :], ACT.Exp).then_inc(exps, 1)
                    nc.scalar.activation(col[1][:, :, :], u[:, :, :], ACT.Exp, scale=ALPHA).then_inc(exps, 1)
                    act.wait_ge(spread, 4)
                    nc.scalar.activation(g.ra[:, 0:T * H], tlow[:, :, :].rearrange("p t h -> p (t h)"), ACT.Exp,
                                         scale=1 - ALPHA).then_inc(exps, 1)
                    nc.scalar.activation(g.rb[:, 0:T * H], thigh[:, :, :].rearrange("p t h -> p (t h)"), ACT.Exp,
                                         scale=ALPHA - 1).then_inc(exps, 1)
                    with act.Fori(0, T // UT) as cc:
                        for side in range(2):
                            n = cc * 2 + side
                            act.wait_ge(wholes, n + 1)
                            nc.scalar.activation(piece(cc, side, 0), unit(whole[side]), ACT.Copy).then_inc(highs, 1)
                            act.wait_ge(rests, n + 3)
                            nc.scalar.activation(piece(cc, side, 1), unit(rest[side]), ACT.Copy).then_inc(mids, 1)

                @block.vector
                def _(dve):
                    dve.sem_inc(rests, 2)
                    s2 = scol[:, :, H:2 * H]
                    nc.vector.tensor_reduce(ends[:, 0:H], s2.rearrange("p t h -> p h t"), AX.X, ALU.max).then_inc(ends_ready, 1)
                    nc.vector.tensor_reduce(ends[:, H:2 * H], s2.rearrange("p t h -> p h t"), AX.X, ALU.min,
                                            negate=True).then_inc(ends_ready, 1)
                    dve.wait_ge(most_ready, 1)
                    nc.vector.tensor_tensor(ends[:, 0:H], most[:, 0:H], most[:, H:2 * H], ALU.add).then_inc(ranged, 1)
                    dve.wait_ge(ranged, 1)
                    nc.vector.tensor_reduce(ends[:, H:H + 1], ends[:, 0:H], AX.X, ALU.max).then_inc(ranged, 1)
                    dve.wait_ge(ranged, 2)
                    nc.vector.tensor_tensor(g.widest[:, :], g.widest[:, :], ends[:, H:H + 1], ALU.max)
                    top = most[:, 0:H].unsqueeze(1).broadcast_to([P, T, H])
                    nc.vector.tensor_tensor(u[:, :, :], s2, top, ALU.subtract).then_inc(spread, 1)
                    nc.vector.tensor_tensor(thigh[:, :, :], scol[:, :, 0:H], top, ALU.add).then_inc(spread, 1)
                    dve.wait_ge(spread, 2)
                    nc.vector.tensor_scalar(tlow[:, :, :], thigh[:, :, :], 0.0, None, ALU.min).then_inc(spread, 1)
                    dve.wait_ge(spread, 3)
                    nc.vector.tensor_scalar(thigh[:, :, :], thigh[:, :, :], 0.0, None, ALU.max).then_inc(spread, 1)
                    nc.vector.tensor_scalar(g.score[:, 0:T * H].rearrange("p (t h) -> p t h", h=H).bitcast(I32),
                                            s2.bitcast(I32), -2, None, ALU.bitwise_and).then_inc(ends_ready, 1)
                    dve.wait_ge(totalled, 1)
                    nc.vector.tensor_copy(g.colsum[:, 0:ROW], ptot[:, 0:ROW]).then_inc(ends_ready, 1)
                    with dve.Fori(0, T // UT) as cc:
                        for side in range(2):
                            n = cc * 2 + side
                            dve.wait_ge(highs, n + 1)
                            dve.wait_ge(wholes, n + 1)
                            nc.vector.tensor_tensor(unit(rest[side]), unit(whole[side]), piece(cc, side, 0),
                                                    ALU.subtract).then_inc(rests, 1)
                            dve.wait_ge(mids, n + 1)
                            nc.vector.tensor_tensor(piece(cc, side, 2), unit(rest[side]), piece(cc, side, 1),
                                                    ALU.subtract).then_inc(lows, 1)
                            dve.wait_ge(lows, n + 1)


def store_for_exact(nc, sem, g, kind, scol, vals, go):
    H, ROW = kind.heads, kind.heads * kind.width
    saved = sem("saved")
    with nc.Block() as plain:
        block = guarded(plain, go)

        @block.sync
        def _(sp):
            for k in range(2):
                for h in range(H):
                    sp.dma_start(g.scores[k, h].rearrange("t p -> p t"), scol[:, :, k * H + h]).then_inc(saved, 16)
            sp.dma_start(g.values[:, 0:T * ROW], vals[:, 0:T * ROW]).then_inc(saved, 16)
            sp.wait_ge(saved, 16 * (2 * H + 1))


def decide(nc, sem, g):
    decided = sem("decided")
    with nc.Block() as block:

        @block.vector
        def _(dve):
            nc.vector.tensor_scalar(g.exact[:, :], g.widest[:, :], WIDEST, None, ALU.is_gt).then_inc(decided, 1)
            dve.wait_ge(decided, 1)


def attend_exact(nc, sem, g, layer, adj, go):
    kind = KINDS[layer]
    H, W = kind.heads, kind.width
    ROW = H * W
    GROUP = 4
    GROUPS = T // GROUP
    LINKS = 6
    adj_in, vals_in, row_in, row_used, shifted = sem("adj_in"), sem("vals_in"), sem("row_in"), sem("row_used"), sem("shifted")
    raised, turned, copied, added = sem("raised"), sem("turned"), sem("copied"), sem("added")
    summed, held, sums_out, chain, stood = sem("summed"), sem("held"), sem("sums_out"), sem("chain"), sem("stood")
    res_free = sem("res_free")
    with ExitStack() as st:
        def sb(name, shape, dt=F32):
            return st.enter_context(nc.sbuf_tensor(f"x{name}_{layer}", shape, dt))

        ints = sb("ints", [P, N], I32)
        edge = sb("edge", [P, N])
        row = sb("row", [P, N])
        e = sb("e", [P, N])
        s1 = sb("s1", [P, H, T])
        vals = sb("vals", [P, T * ROW])
        top, ntop = sb("top", [P, 1]), sb("ntop", [P, 1])
        pt = [sb(f"pt{b}", [P, GROUP * P]) for b in range(2)]
        res = sb("res", [P, W])
        turn = [st.enter_context(nc.psum_tensor(f"xturn{b}_{layer}", [P, GROUP * P], F32)) for b in range(2)]
        acc = st.enter_context(nc.psum_tensor(f"xacc_{layer}", [P, BANK], F32))
        with nc.Block() as plain:
            block = guarded(plain, go)

            @block.sync
            def _(sp):
                sp.sem_inc(res_free, 1)
                sp.dma_start(vals[:, :], g.values[:, 0:T * ROW]).then_inc(vals_in, 16)
                for h in range(H):
                    sp.dma_start(s1[:, h, :], g.scores[0, h].rearrange("t p -> p t")).then_inc(vals_in, 16)
                for h in range(H):
                    if h:
                        sp.wait_ge(row_used, h * T)
                    src = g.scores[1, h].rearrange("t p -> (t p)").unsqueeze(0).broadcast_to([P, N])
                    sp.dma_start(row[:, :], src).then_inc(row_in, 16)
                    with sp.Fori(0, T) as it:
                        n = it + h * T
                        sp.wait_ge(chain, n * LINKS + 1)
                        sp.dma_start(ints[:, :], adj[bass.ds(it * P, P), :]).then_inc(adj_in, 16)
                        sp.wait_ge(held, n + 1)
                        if layer < 3:
                            dst = g.sums[layer][bass.ds(it, 1), :, h * W:(h + 1) * W].rearrange("a p w -> (a p) w")
                        else:
                            dst = g.sums[layer][h, bass.ds(it * P, P), :]
                        sp.dma_start(dst, res[:, :]).then_inc(sums_out, 16)
                        sp.wait_ge(sums_out, (n + 1) * 16)
                        sp.sem_inc(res_free, 1)

            @block.vector
            def _(dve):
                dve.sem_inc(chain, LINKS)
                dve.wait_ge(vals_in, 16 * (1 + H))
                for h in range(H):
                    dve.wait_ge(row_in, 16 * (h + 1))
                    with dve.Fori(0, T) as it:
                        n = it + h * T
                        made = [0]

                        def link(ins):
                            made[0] += 1
                            ins.then_inc(chain, 1)
                            dve.wait_ge(chain, (n + 1) * LINKS + made[0])

                        dve.wait_ge(adj_in, (n + 1) * 16)
                        link(nc.vector.tensor_scalar(edge[:, :], ints[:, :], 0, None, ALU.is_gt))
                        dve.wait_ge(summed, n + 1)
                        nc.vector.tensor_scalar(e[:, :], row[:, :], s1[:, h, bass.ds(it, 1)], None,
                                                ALU.add).then_inc(row_used, 1)
                        dve.wait_ge(row_used, n + 1)
                        link(nc.vector.scalar_tensor_tensor(e[:, :], e[:, :], ALPHA, e[:, :], ALU.mult, ALU.max))
                        link(nc.vector.tensor_tensor(e[:, :], e[:, :], edge[:, :], ALU.mult))
                        link(nc.vector.tensor_scalar(edge[:, :], edge[:, :], -1.0, -NEG_INF, ALU.add, ALU.mult))
                        link(nc.vector.tensor_tensor(e[:, :], e[:, :], edge[:, :], ALU.add))
                        link(nc.vector.tensor_reduce(top[:, :], e[:, :], AX.X, ALU.max))
                        nc.vector.tensor_scalar(ntop[:, :], top[:, :], -1.0, None, ALU.mult).then_inc(shifted, 1)

            @block.scalar
            def _(act):
                with act.Fori(0, H * T) as n:
                    act.wait_ge(shifted, n + 1)
                    nc.scalar.activation(e[:, :], e[:, :], ACT.Exp, bias=ntop[:, :]).then_inc(raised, 1)
                    with act.Fori(0, GROUPS // 2) as j:
                        for b in range(2):
                            k = n * GROUPS + j * 2 + b
                            act.wait_ge(turned, k + 1)
                            act.wait_ge(added, k + 1)
                            nc.scalar.activation(pt[b][:, :], turn[b][:, :], ACT.Copy).then_inc(copied, 1)
                    act.wait_ge(summed, n + 2)
                    act.wait_ge(res_free, n + 1)
                    nc.scalar.activation(res[:, :], acc[:, 0:W], ACT.Copy).then_inc(held, 1)

            @block.tensor
            def _(pe):
                pe.sem_inc(summed, 1)
                pe.sem_inc(added, 2)
                pe.wait_ge(vals_in, 16 * (1 + H))
                with pe.Fori(0, H) as h:
                    with pe.Fori(0, T) as it:
                        n = it + h * T
                        pe.wait_ge(raised, n + 1)
                        nc.tensor.matmul(acc[:, 0:2], g.zeros[:, :], g.zeros[:, 0:2], start=True, stop=False,
                                         skip_group_check=True)
                        for j in range(GROUPS):
                            for t in range(GROUP):
                                at = (j * GROUP + t) * P
                                last = nc.tensor.transpose(turn[j % 2][:, t * P:(t + 1) * P], e[:, at:at + P],
                                                           g.identf[:, :])
                            last.then_inc(turned, 1)
                            pe.wait_ge(copied, n * GROUPS + (j + 1))
                            for t in range(GROUP):
                                rhs = vals[:, bass.ds(h * W + (j * GROUP + t) * ROW, W)]
                                last = nc.tensor.matmul(acc[:, 0:W], pt[j % 2][:, t * P:(t + 1) * P], rhs,
                                                        start=False, stop=False, skip_group_check=True)
                            last.then_inc(added, 1)
                        nc.tensor.matmul(acc[:, 0:2], g.zeros[:, :], g.zeros[:, 0:2], start=False, stop=True,
                                         skip_group_check=True).then_inc(summed, 1)


def attend_one(nc, sem, g, layer):
    W = F + 1
    W3 = PIECES * W
    R, J, LT = 512, 4, 8
    NB = R // P
    BLOCKS = N // R
    STEPS_LOAD = LT // J
    LOOPS = T // (2 * LT)
    STEPS_ITER = 2 * STEPS_LOAD
    STEPS = LOOPS * STEPS_ITER
    SIGNS = 4
    WIDE = J * R
    adj_in = [sem("adj_in0"), sem("adj_in1")]
    row_in = [sem("row_in0"), sem("row_in1")]
    signs, edges, masks, used = sem("signs"), sem("edges"), sem("masks"), sem("used")
    acc_ready, acc_free, sums_used, chain = sem("acc_ready"), sem("acc_free"), sem("sums_used"), sem("chain")
    stood = sem("stood")
    with ExitStack() as st:
        def sb(name, shape, dt=F32):
            return st.enter_context(nc.sbuf_tensor(f"{name}_{layer}", shape, dt))

        adj = [sb(f"adj{q}", [P, LT, IBLK], BF16) for q in range(2)]
        row = [sb(f"row{q}", [P, R]) for q in range(2)]
        sgn = [sb(f"sgn{q}", [P, WIDE], BF16) for q in range(SIGNS)]
        mask = [[sb(f"mask{q}{s}", [P, WIDE], BF16) for s in range(2)] for q in range(2)]
        acc = st.enter_context(nc.psum_tensor(f"acc_{layer}", [P, 8, BANK], F32))
        raw = sb("raw", [P, 8, W3])
        tot = sb("tot", [P, NB * 2, W])
        res, tmp = sb("res", [P, NB, W]), sb("tmp", [P, NB, W])
        flag = sb("flag", [P, NB])
        with nc.Block() as block:

            @block.sync
            def _(sp):
                with sp.Fori(0, BLOCKS // 2) as bb:
                    for par in range(2):
                        blk = bb * 2 + par
                        sp.wait_ge(signs, (blk + 1) * STEPS)
                        src = g.rows1[0:1, bass.ds(blk * R, R)]
                        sp.dma_start(row[par][:, :], src.broadcast_to([P, R])).then_inc(row_in[par], 16)
                        with sp.Fori(0, LOOPS) as j:
                            for q in range(2):
                                load = (blk * LOOPS + j) * 2 + q
                                sp.wait_ge(edges, (load + 1) * STEPS_LOAD)
                                src = g.adj_t[bass.ds(blk, 1), :, bass.ds((j * 2 + q) * LT, LT), :]
                                sp.dma_start(adj[q][:, :, :], src.rearrange("s p t i -> p (s t) i")).then_inc(adj_in[q], 16)

            @block.scalar
            def _(act):
                act.sem_inc(signs, 2 * STEPS)
                with act.Fori(0, BLOCKS // 2) as bb:
                    for par in range(2):
                        blk = bb * 2 + par
                        act.wait_ge(row_in[par], (bb + 1) * 16)
                        with act.Fori(0, LOOPS) as j:
                            for k in range(STEPS_ITER):
                                n = (blk * LOOPS + j) * STEPS_ITER + k
                                act.wait_ge(masks, n + 1)
                                for t in range(J):
                                    col = (j * STEPS_ITER + k) * J + t
                                    last = nc.scalar.activation(sgn[k % SIGNS][:, t * R:(t + 1) * R], row[par][:, :],
                                                                ACT.Sign, bias=g.score[:, bass.ds(col, 1)])
                                last.then_inc(signs, 1)

            @block.vector
            def _(dve):
                dve.sem_inc(edges, 2 * STEPS_LOAD)
                dve.sem_inc(masks, SIGNS)

                def split_signs(it, k):
                    n = it * STEPS_ITER + k
                    dve.wait_ge(used, n + 1)
                    dve.wait_ge(edges, n + (1 + 2 * STEPS_LOAD))
                    nc.vector.tensor_scalar(mask[k % 2][1][:, :], sgn[k % SIGNS][:, :], 0.0, None, ALU.max)
                    nc.vector.tensor_scalar(mask[k % 2][0][:, :], sgn[k % SIGNS][:, :], -1.0, 0.0,
                                            ALU.mult, ALU.max).then_inc(masks, 1)

                def steps(it, evacuate=None):
                    for k in range(STEPS_ITER):
                        n = it * STEPS_ITER + k
                        q, kk = k // STEPS_LOAD, k % STEPS_LOAD
                        if kk == 0:
                            dve.wait_ge(adj_in[q], (it + 1) * 16)
                        dve.wait_ge(signs, n + (1 + 2 * STEPS))
                        s = sgn[k % SIGNS][:, :]
                        a = adj[q][:, kk * J:(kk + 1) * J, :].rearrange("p t i -> p (t i)")
                        nc.vector.tensor_tensor(s, s, a, ALU.mult).then_inc(edges, 1)
                        if k:
                            split_signs(it, k - 1)
                        if k == 2 and evacuate:
                            evacuate()
                    split_signs(it, STEPS_ITER - 1)

                def sums_out(blk):
                    dve.wait_ge(sums_used, blk + 1)
                    for b in range(8):
                        dve.wait_ge(acc_ready, blk * 8 + (b + 1))
                        nc.vector.tensor_copy(raw[:, b, :], acc[:, b, 0:W3]).then_inc(acc_free, 1)

                with dve.Fori(0, BLOCKS) as blk:
                    steps(blk * LOOPS, lambda: sums_out(blk))
                    with dve.Fori(1, LOOPS) as j:
                        steps(blk * LOOPS + j)
                sums_out(BLOCKS)

            @block.tensor
            def _(pe):
                pe.sem_inc(used, 2)
                for b in range(8):
                    zero_bank(nc, g, acc, b, W3).then_inc(acc_ready, 1)

                def add(k, tile, t, b, first):
                    for s in range(2):
                        rhs = g.split[:, bass.ds((tile + t) * (2 * W3) + s * W3, W3)]
                        last = nc.tensor.matmul(acc[:, 2 * b + s, 0:W3], mask[k % 2][s][:, t * R + b * P:t * R + (b + 1) * P],
                                                rhs, start=first, stop=False, skip_group_check=True)
                    return last

                with pe.Fori(0, BLOCKS) as blk:
                    def steps(j, opening=False):
                        for k in range(STEPS_ITER):
                            n = (blk * LOOPS + j) * STEPS_ITER + k
                            tile = (j * STEPS_ITER + k) * J
                            pe.wait_ge(masks, n + (1 + SIGNS))
                            for b in range(NB):
                                first = opening and k == 0
                                if first:
                                    pe.wait_ge(acc_free, blk * 8 + (2 * b + 2))
                                for t in range(J):
                                    last = add(k, tile, t, b, first and t == 0)
                            last.then_inc(used, 1)

                    steps(0, opening=True)
                    with pe.Fori(1, LOOPS) as j:
                        steps(j)
                    for b in range(8):
                        close_bank(nc, g, acc, b).then_inc(acc_ready, 1)

            @block.gpsimd
            def _(pool):
                pool.sem_inc(sums_used, 1)
                pool.wait_ge(acc_free, 8)
                pool.sem_inc(sums_used, 1)
                LINKS = 7
                before = g.pool_stores
                g.pool_stores += 16 * BLOCKS
                with pool.Fori(0, BLOCKS) as blk:
                    made = [0]

                    def link(ins):
                        made[0] += 1
                        ins.then_inc(chain, 1)
                        pool.wait_ge(chain, blk * LINKS + made[0])

                    def factor(v):
                        return v[:, bass.ds(blk * NB, NB)].unsqueeze(2).broadcast_to([P, NB, W])

                    pool.wait_ge(acc_free, blk * 8 + 16)
                    r = raw[:, :, :].rearrange("p b (q w) -> p b q w", w=W)
                    link(nc.gpsimd.tensor_tensor(tot[:, :, :], r[:, :, 0, :], r[:, :, 1, :], ALU.add))
                    nc.gpsimd.tensor_tensor(tot[:, :, :], tot[:, :, :], r[:, :, 2, :], ALU.add).then_inc(sums_used, 1)
                    pool.wait_ge(sums_used, blk + 3)
                    two = tot[:, :, :].rearrange("p (u s) w -> p u s w", s=2)
                    link(nc.gpsimd.tensor_tensor(res[:, :, :], two[:, :, 0, :], factor(g.ra), ALU.mult))
                    link(nc.gpsimd.tensor_tensor(tmp[:, :, :], two[:, :, 1, :], factor(g.rb), ALU.mult))
                    link(nc.gpsimd.tensor_tensor(res[:, :, :], res[:, :, :], tmp[:, :, :], ALU.add))
                    pool.sem_inc(stood, 1)
                    link(nc.gpsimd.tensor_scalar(flag[:, :], res[:, :, W - 1], 0.0, None, ALU.is_equal))
                    link(nc.gpsimd.tensor_tensor(tmp[:, :, :], flag[:, :].unsqueeze(2).broadcast_to([P, NB, W]),
                                                 g.colsum[:, 0:W].unsqueeze(1).broadcast_to([P, NB, W]), ALU.mult))
                    link(nc.gpsimd.tensor_tensor(res[:, :, :], res[:, :, :], tmp[:, :, :], ALU.add))
                    dst = g.sums[layer][bass.ds(blk * NB, NB)]
                    pool.dma_start(dst.rearrange("b p w -> p b w"), res[:, :, :]).then_inc(g.pool_stored, 16)
                    pool.wait_ge(g.pool_stored, (blk + 1) * 16 + before)
                    pool.sem_inc(stood, 1)


def zero_bank(nc, g, acc, b, width):
    return nc.tensor.matmul(acc[:, b, 0:width], g.zeros[:, :], g.zeros[:, 0:1].broadcast_to([P, width]),
                            start=True, stop=True, skip_group_check=True)


def close_bank(nc, g, acc, b):
    return nc.tensor.matmul(acc[:, b, 0:2], g.zeros[:, :], g.zeros[:, 0:2], start=False, stop=True,
                            skip_group_check=True)


def attend_four(nc, sem, g, layer):
    H, W, PH, PASSES = 4, F // 4 + 1, 2, 2
    W3 = PIECES * W
    PAIR = 4 * W3
    R, LT = 1024, 4
    NB = R // P
    BLOCKS = N // R
    SUB = R // IBLK
    STEPS_ITER = 2 * LT
    LOOPS = T // STEPS_ITER
    STEPS = T
    BUFS = 4
    WIDE = PH * R
    HELD = 2 * LT
    adj_in = [sem("adj_in0"), sem("adj_in1")]
    row_in = [sem("row_in0"), sem("row_in1")]
    signs, masks, used = sem("signs"), sem("masks"), sem("used")
    acc_ready, acc_free, sums_used, chain = sem("acc_ready"), sem("acc_free"), sem("sums_used"), sem("chain")
    stood = sem("stood")
    with ExitStack() as st:
        def sb(name, shape, dt=F32):
            return st.enter_context(nc.sbuf_tensor(f"{name}_{layer}", shape, dt))

        adj = [sb(f"adj{q}", [P, SUB, LT, IBLK], BF16) for q in range(2)]
        row = [sb(f"row{q}", [P, PH, R]) for q in range(2)]
        sgn = [sb(f"sgn{q}", [P, WIDE], BF16) for q in range(BUFS)]
        mask = [sb(f"mask{q}", [P, WIDE], BF16) for q in range(BUFS)]
        acc = st.enter_context(nc.psum_tensor(f"acc_{layer}", [P, 8, BANK], F32))
        raw = sb("raw", [P, 8, PAIR])
        tot = sb("tot", [P, NB * 4, W])
        res, tmp = sb("res", [P, NB * PH, W]), sb("tmp", [P, NB * PH, W])
        flag = sb("flag", [P, NB * PH])
        with nc.Block() as block:

            @block.sync
            def _(sp):
                for ps in range(PASSES):
                    with sp.Fori(0, BLOCKS // 2) as bb:
                        for par in range(2):
                            blk = bb * 2 + par
                            done = ps * BLOCKS
                            sp.wait_ge(signs, (blk + (done + 1)) * STEPS)
                            src = g.rows1[ps * PH:(ps + 1) * PH, bass.ds(blk * R, R)]
                            sp.dma_start(row[par][:, :, :], src.unsqueeze(0).broadcast_to([P, PH, R])).then_inc(row_in[par], 16)
                            with sp.Fori(0, LOOPS) as j:
                                for q in range(2):
                                    load = ((blk + done) * LOOPS + j) * 2 + q
                                    sp.wait_ge(used, (load + 1) * LT)
                                    src = g.adj_t[bass.ds(blk * SUB, SUB), :, bass.ds((j * 2 + q) * LT, LT), :]
                                    src = src.rearrange("s p t i -> p s t i")
                                    sp.dma_start(adj[q][:, :, :, :], src).then_inc(adj_in[q], 16)

            @block.scalar
            def _(act):
                act.sem_inc(signs, 2 * STEPS)
                for ps in range(PASSES):
                    with act.Fori(0, BLOCKS // 2) as bb:
                        for par in range(2):
                            blk = bb * 2 + par + ps * BLOCKS
                            act.wait_ge(row_in[par], (bb + (ps * (BLOCKS // 2) + 1)) * 16)
                            with act.Fori(0, LOOPS) as j:
                                for k in range(STEPS_ITER):
                                    n = (blk * LOOPS + j) * STEPS_ITER + k
                                    act.wait_ge(masks, n + 1)
                                    for h in range(PH):
                                        col = (j * STEPS_ITER + k) * H + (ps * PH + h)
                                        last = nc.scalar.activation(sgn[k % BUFS][:, h * R:(h + 1) * R], row[par][:, h, :],
                                                                    ACT.Sign, bias=g.score[:, bass.ds(col, 1)])
                                    last.then_inc(signs, 1)

            @block.vector
            def _(dve):
                dve.sem_inc(masks, BUFS)

                def steps(it, evacuate=None):
                    for k in range(STEPS_ITER):
                        n = it * STEPS_ITER + k
                        q, kk = k // LT, k % LT
                        if kk == 0:
                            dve.wait_ge(adj_in[q], (it + 1) * 16)
                        dve.wait_ge(signs, n + (1 + 2 * STEPS))
                        dve.wait_ge(used, n + (1 + HELD - BUFS))
                        x = sgn[k % BUFS][:, :].rearrange("p (h s i) -> p h s i", h=PH, s=SUB)
                        m = mask[k % BUFS][:, :].rearrange("p (h s i) -> p h s i", h=PH, s=SUB)
                        a = adj[q][:, :, kk, :].unsqueeze(1).broadcast_to([P, PH, SUB, IBLK])
                        nc.vector.tensor_tensor(m, x, a, ALU.is_equal).then_inc(masks, 1)
                        if k == BUFS - 2 and evacuate:
                            evacuate()

                def sums_out(blk):
                    dve.wait_ge(sums_used, blk + 1)
                    for b in range(8):
                        dve.wait_ge(acc_ready, blk * 8 + (b + 1))
                        nc.vector.tensor_copy(raw[:, b, :], acc[:, b, 0:PAIR]).then_inc(acc_free, 1)

                with dve.Fori(0, PASSES * BLOCKS) as blk:
                    steps(blk * LOOPS, lambda: sums_out(blk))
                    with dve.Fori(1, LOOPS) as j:
                        steps(blk * LOOPS + j)
                sums_out(PASSES * BLOCKS)

            @block.tensor
            def _(pe):
                pe.sem_inc(used, HELD)
                for b in range(8):
                    zero_bank(nc, g, acc, b, PAIR).then_inc(acc_ready, 1)
                for ps in range(PASSES):
                    with pe.Fori(0, BLOCKS) as bb:
                        blk = bb + ps * BLOCKS

                        def steps(j, opening=False):
                            for k in range(STEPS_ITER):
                                n = (blk * LOOPS + j) * STEPS_ITER + k
                                pe.wait_ge(masks, n + (1 + BUFS))
                                first = opening and k == 0
                                at = (j * STEPS_ITER + k) * (2 * PAIR) + ps * PAIR
                                for b in range(NB):
                                    if first:
                                        pe.wait_ge(acc_free, blk * 8 + (b + 1))
                                    for h in range(PH):
                                        nc.tensor.matmul(acc[:, b, h * 2 * W3:(h + 1) * 2 * W3],
                                                         mask[k % BUFS][:, h * R + b * P:h * R + (b + 1) * P],
                                                         g.split[:, bass.ds(at + h * 2 * W3, 2 * W3)],
                                                         start=first and h == 0, stop=False, skip_group_check=True)
                                    i = b * P % IBLK
                                    last = nc.tensor.matmul(acc[:, b, W3:3 * W3], adj[k // LT][:, b * P // IBLK, k % LT, i:i + P],
                                                            g.split[:, bass.ds(at + W3, 2 * W3)],
                                                            start=False, stop=False, skip_group_check=True)
                                last.then_inc(used, 1)

                        steps(0, opening=True)
                        with pe.Fori(1, LOOPS) as j:
                            steps(j)
                        for b in range(8):
                            close_bank(nc, g, acc, b).then_inc(acc_ready, 1)

            @block.gpsimd
            def _(pool):
                pool.sem_inc(sums_used, 1)
                pool.wait_ge(acc_free, 8)
                pool.sem_inc(sums_used, 1)
                LINKS = 7
                each = 16 if layer < 3 else 16 * PH
                before = g.pool_stores
                g.pool_stores += each * PASSES * BLOCKS
                for ps in range(PASSES):
                    with pool.Fori(0, BLOCKS) as bb:
                        blk = bb + ps * BLOCKS
                        made = [0]

                        def link(ins):
                            made[0] += 1
                            ins.then_inc(chain, 1)
                            pool.wait_ge(chain, blk * LINKS + made[0])

                        def heads(v):
                            return v.rearrange("p (b h) w -> p b h w", h=PH)

                        def factor(v):
                            v = v[:, bass.ds(bb * (NB * H), NB * H)].rearrange("p (b h) -> p b h", h=H)
                            return v[:, :, ps * PH:(ps + 1) * PH].unsqueeze(3).broadcast_to([P, NB, PH, W])

                        pool.wait_ge(acc_free, blk * 8 + 16)
                        r = raw[:, :, :].rearrange("p b (c q w) -> p (b c) q w", c=4, q=PIECES)
                        link(nc.gpsimd.tensor_tensor(tot[:, :, :], r[:, :, 0, :], r[:, :, 1, :], ALU.add))
                        nc.gpsimd.tensor_tensor(tot[:, :, :], tot[:, :, :], r[:, :, 2, :], ALU.add).then_inc(sums_used, 1)
                        pool.wait_ge(sums_used, blk + 3)
                        four = tot[:, :, :].rearrange("p (b c) w -> p b c w", c=4)
                        link(nc.gpsimd.tensor_tensor(heads(res[:, :, :]), four[:, :, 0:4:3, :], factor(g.rb), ALU.mult))
                        link(nc.gpsimd.tensor_tensor(heads(tmp[:, :, :]), four[:, :, 1:3, :], factor(g.ra), ALU.mult))
                        link(nc.gpsimd.tensor_tensor(res[:, :, :], res[:, :, :], tmp[:, :, :], ALU.subtract))
                        pool.sem_inc(stood, 1)
                        link(nc.gpsimd.tensor_scalar(flag[:, :], res[:, :, W - 1], 0.0, None, ALU.is_equal))
                        cs = g.colsum[:, ps * PH * W:(ps + 1) * PH * W]
                        cs = cs.rearrange("p (h w) -> p h w", h=PH).unsqueeze(1).broadcast_to([P, NB, PH, W])
                        fl = flag[:, :].rearrange("p (b h) -> p b h", h=PH).unsqueeze(3).broadcast_to([P, NB, PH, W])
                        link(nc.gpsimd.tensor_tensor(heads(tmp[:, :, :]), fl, cs, ALU.mult))
                        link(nc.gpsimd.tensor_tensor(res[:, :, :], res[:, :, :], tmp[:, :, :], ALU.add))
                        if layer < 3:
                            dst = g.sums[layer][bass.ds(bb * NB, NB), :, ps * PH * W:(ps + 1) * PH * W]
                            pool.dma_start(dst.rearrange("b p w -> p b w"),
                                           res[:, :, :].rearrange("p (b h) w -> p b (h w)", h=PH)).then_inc(g.pool_stored, 16)
                        else:
                            for h in range(PH):
                                dst = g.sums[layer][ps * PH + h, bass.ds(bb * R, R), :]
                                pool.dma_start(dst.rearrange("(b p) w -> p b w", p=P),
                                               heads(res[:, :, :])[:, :, h, :]).then_inc(g.pool_stored, 16)
                        pool.wait_ge(g.pool_stored, (blk + 1) * each + before)
                        pool.sem_inc(stood, 1)


def gat_kernel(nc, x, adj, L0_W, L0_a1, L0_a2, L1_W, L1_a, L2_W, L2_a, L3_W, L3_a, out):
    D = F // 4
    one = lambda v: v.rearrange("(h d) -> h d", h=1)
    weights = [
        (L0_W, one(L0_a1), one(L0_a2)),
        (L1_W, L1_a[0, :, 0:D], L1_a[0, :, D:2 * D]),
        (L2_W, L2_a[0:F, :].rearrange("d h -> h d"), L2_a[F:2 * F, :].rearrange("d h -> h d")),
        (L3_W, L3_a[:, D:2 * D, 0], L3_a[:, 0:D, 0]),
    ]
    with ExitStack() as ctx:
        ctx.enter_context(nc.allow_non_contiguous_dma("weights"))
        g = tensors(nc, ctx)
        with stage_semaphores(nc, "setup") as sem:
            setup(nc, sem, g, weights)
        with ExitStack() as factored:
            g.split = factored.enter_context(nc.sbuf_tensor("split", [P, T * STAT_MAX], BF16))
            with stage_semaphores(nc, "turn") as sem:
                transpose_adjacency(nc, sem, g, adj)
            for layer in range(4):
                with stage_semaphores(nc, f"nodes{layer}") as sem:
                    update_nodes(nc, sem, g, layer, x, out)
                with stage_semaphores(nc, f"attend{layer}") as sem:
                    (attend_one if KINDS[layer].heads == 1 else attend_four)(nc, sem, g, layer)
            with stage_semaphores(nc, "nodes4") as sem:
                update_nodes(nc, sem, g, 4, x, out)
        with stage_semaphores(nc, "decide") as sem:
            decide(nc, sem, g)
        go = nc.values_load(g.exact[0:1, 0:1], min_val=0, max_val=1)
        for layer in range(4):
            with stage_semaphores(nc, f"xnodes{layer}") as sem:
                update_nodes(nc, sem, g, layer, x, out, go)
            with stage_semaphores(nc, f"xattend{layer}") as sem:
                attend_exact(nc, sem, g, layer, adj, go)
        with stage_semaphores(nc, "xnodes4") as sem:
            update_nodes(nc, sem, g, 4, x, out, go)


_INS = ["x", "adj", "L0_gnn_W", "L0_gnn_a1", "L0_gnn_a2", "L1_gnn_W", "L1_gnn_a", "L2_gnn_W", "L2_gnn_a",
        "L3_gnn_W", "L3_gnn_a"]


def kernel(**inputs):
    import numpy as _np
    import concourse.bacc as _bacc
    from concourse import mybir as _mybir
    from concourse.bass_utils import run_bass_kernel_spmd as _run

    nc = _bacc.Bacc("TRN2", target_bir_lowering=False, num_devices=1)
    arrays, args = {}, []
    for name in _INS:
        a = _np.ascontiguousarray(inputs[name])
        arrays[f"in_{name}"] = a
        args.append(nc.dram_tensor(f"in_{name}", a.shape, _mybir.dt.from_np(a.dtype), kind="ExternalInput").ap())
    args.append(nc.dram_tensor("out_nodes", (N, F), F32, kind="ExternalOutput").ap())
    gat_kernel(nc, *args)
    r = _run(nc, [arrays], core_ids=[0])
    return r.results[0]["out_nodes"]
```

```python
from contextlib import ExitStack, contextmanager

import concourse.bass as bass
from concourse import mybir

F32 = mybir.dt.float32
BF16 = mybir.dt.bfloat16
I32 = mybir.dt.int32
ALU = mybir.AluOpType
ACT = mybir.ActivationFunctionType
AX = mybir.AxisListType
RMAX = bass.bass_isa.ReduceOp.max

P = 128
N = 8192
F = 128
T = N // P
ALPHA = 0.2
EPS = 1e-5
BANK = 512
PIECES = 3
IBLK = 512
NEG_INF = -9000000000000000.0
WIDEST = 60.0
TINY = 2.0 ** -60


class Kind:

    def __init__(self, heads):
        self.heads, self.width = heads, F // heads + 1


class Guarded:

    def __init__(self, sync, scalar, vector, tensor, gpsimd):
        self.sync, self.scalar, self.vector, self.tensor, self.gpsimd = sync, scalar, vector, tensor, gpsimd


class Shared:
    pass


KINDS = [Kind(1), Kind(4), Kind(1), Kind(4)]
ROW_MAX = max(k.heads * k.width for k in KINDS)
STAT_MAX = max(2 * k.heads * PIECES * k.width for k in KINDS)
AUG = F + 2 * 4


def guarded(block, go):
    if go is None:
        return block

    def only_if(attach):
        def take(program):
            def body(engine):
                with engine.If(go > 0):
                    program(engine)
                with engine.Else():
                    engine.nop()

            attach(body)

        return take

    return Guarded(sync=only_if(block.sync), scalar=only_if(block.scalar), vector=only_if(block.vector),
                           tensor=only_if(block.tensor), gpsimd=only_if(block.gpsimd))


@contextmanager
def stage_semaphores(nc, tag):
    with ExitStack() as st:
        made = []

        def sem(name):
            made.append(st.enter_context(nc.semaphore(f"{tag}_{name}")))
            return made[-1]

        yield sem
        with nc.Block() as block:

            @block.gpsimd
            def _(pool):
                for s in made:
                    pool.sem_clear(s)


def tensors(nc, ctx):
    def sb(name, shape, dt):
        return ctx.enter_context(nc.sbuf_tensor(name, shape, dt))

    g = Shared()
    g.identf = sb("identf", [P, P], F32)
    g.identb = sb("identb", [P, P], BF16)
    g.zeros = sb("zeros", [P, P], BF16)
    g.onesf = sb("onesf", [P, P], F32)
    g.waug = sb("waug", [P, 4, AUG], F32)
    g.widest = sb("widest", [P, 1], F32)
    g.exact = sb("exact", [P, 1], I32)
    g.score = sb("score", [P, T * 4], F32)
    g.ra = sb("ra", [P, T * 4], F32)
    g.rb = sb("rb", [P, T * 4], F32)
    g.colsum = sb("colsum", [P, ROW_MAX], F32)
    g.adj_t = nc.dram_tensor("adj_t", [N // IBLK, P, T, IBLK], BF16, kind="Internal").ap()
    g.scores = nc.dram_tensor("scores", [2, 4, T, P], F32, kind="Internal").ap()
    g.values = nc.dram_tensor("values", [P, T * ROW_MAX], F32, kind="Internal").ap()
    g.nodes = nc.dram_tensor("nodes", [N, F], F32, kind="Internal").ap()
    g.rows1 = nc.dram_tensor("rows1", [4, N], F32, kind="Internal").ap()
    g.sums = [nc.dram_tensor(f"sums{l}", [T, P, k.heads * k.width] if l < 3 else [k.heads, N, k.width], F32,
                             kind="Internal").ap() for l, k in enumerate(KINDS)]
    g.pool_stored = ctx.enter_context(nc.semaphore("pool_stored"))
    g.pool_stores = 0
    return g


def setup(nc, sem, g, weights):
    blank, weights_in, made, summed = sem("blank"), sem("weights_in"), sem("made"), sem("summed")
    with ExitStack() as st:
        vecs = st.enter_context(nc.sbuf_tensor("vecs", [P, 4, 2, F], F32))
        prod = st.enter_context(nc.sbuf_tensor("prod", [P, 4, 2, F], F32))
        with nc.Block() as block:

            @block.sync
            def _(sp):
                for l, (w, score_i, score_j) in enumerate(weights):
                    if len(w.shape) == 3:
                        dst = g.waug[:, l, 0:F].rearrange("p (h d) -> p h d", h=w.shape[0])
                        sp.dma_start(dst, w.rearrange("h p d -> p h d")).then_inc(weights_in, 16)
                    else:
                        sp.dma_start(g.waug[:, l, 0:F], w).then_inc(weights_in, 16)
                    for k, a in enumerate((score_i, score_j)):
                        h, d = a.shape
                        dst = vecs[:, l, k, :].rearrange("p (h d) -> p h d", h=h)
                        sp.dma_start(dst, a.unsqueeze(0).broadcast_to([P, h, d])).then_inc(weights_in, 16)

            @block.gpsimd
            def _(pool):
                nc.gpsimd.memset(g.identf[:, :], 0.0).then_inc(blank, 1)
                nc.gpsimd.memset(g.identb[:, :], 0.0).then_inc(blank, 1)
                nc.gpsimd.memset(g.zeros[:, :], 0.0).then_inc(blank, 1)
                nc.gpsimd.memset(g.onesf[:, :], 1.0).then_inc(blank, 1)
                nc.gpsimd.memset(g.widest[:, :], 0.0)
                pool.wait_ge(blank, 4)
                for m in (g.identf, g.identb):
                    nc.gpsimd.affine_select(out=m[:, :], in_=m[:, :], compare_op=ALU.not_equal, fill=1.0,
                                            base=0, pattern=[[-1, P]], channel_multiplier=1).then_inc(blank, 1)

            @block.vector
            def _(dve):
                dve.wait_ge(weights_in, 16 * 12)
                for l in range(4):
                    nc.vector.tensor_tensor(prod[:, l], vecs[:, l],
                                            g.waug[:, l, 0:F].unsqueeze(1).broadcast_to([P, 2, F]),
                                            ALU.mult).then_inc(made, 1)
                dve.wait_ge(made, 4)
                for l, k in enumerate(KINDS):
                    dst = g.waug[:, l, F:F + 2 * k.heads].rearrange("p (k h) -> p k h", k=2)
                    src = prod[:, l].rearrange("p k (h d) -> p k h d", h=k.heads)
                    nc.vector.tensor_reduce(dst, src, AX.X, ALU.add).then_inc(summed, 1)


def attend_and_transpose(nc, sem, g, adj):
    W = F + 1
    W3 = PIECES * W
    R, COLS = 256, 1024
    NB, J = R // P, COLS // P
    BLOCKS, STEPS = N // R, N // COLS
    RING = 4
    BANKS = 2 * NB
    TURN = J * R // (2 * BANK)
    int_in = [sem(f"int_in{q}") for q in range(RING)]
    row_in = [sem("row_in0"), sem("row_in1")]
    converted, turned, packed = sem("converted"), sem("turned"), sem("packed")
    stored = [sem(f"stored{q}") for q in range(RING)]
    edges, masks, used = sem("edges"), sem("masks"), sem("used")
    acc_ready, acc_free, sums_used, chain = sem("acc_ready"), sem("acc_free"), sem("sums_used"), sem("chain")
    stood = sem("stood")

    def over_blocks(engine, program):
        program(0, 0, True)
        program(0, 1, False)
        with engine.Fori(1, BLOCKS // 2) as pair:
            program(pair, 0, False)
            program(pair, 1, False)

    with ExitStack() as st:
        def sb(name, shape, dt=F32):
            return st.enter_context(nc.sbuf_tensor(f"{name}_0", shape, dt))

        ints = [sb(f"ints{q}", [P, NB, COLS], I32) for q in range(RING)]
        ones = [sb(f"ones{q}", [P, NB, COLS], BF16) for q in range(2)]
        pack = [sb(f"pack{q}", [P, J, R], BF16) for q in range(RING)]
        row = [sb(f"row{q}", [P, R]) for q in range(2)]
        sgn = [sb(f"sgn{q}", [P, J * R], BF16) for q in range(RING)]
        mask = [[sb(f"mask{q}{s}", [P, J * R], BF16) for s in range(2)] for q in range(2)]
        acc = st.enter_context(nc.psum_tensor("acc_0", [P, BANKS, BANK], F32))
        turn = st.enter_context(nc.psum_tensor("turn", [P, 2, J * R], BF16))
        raw = sb("raw", [P, BANKS, W3])
        tot = sb("tot", [P, BANKS, W])
        res, tmp = sb("res", [P, NB, W]), sb("tmp", [P, NB, W])
        flag = sb("flag", [P, NB])
        with nc.Block() as block:

            @block.sync
            def _(sp):
                def store(pair, par, k):
                    sp.wait_ge(packed, (pair * 2 + par) * STEPS + (k + 1))
                    dst = g.adj_t[bass.ds(pair, 1), :, k * J:(k + 1) * J, par * R:(par + 1) * R]
                    sp.dma_start(dst.rearrange("b p t i -> (b p) t i"), pack[k % RING][:, :, :]).then_inc(stored[k % RING], 16)

                def program(pair, par, first):
                    blk = pair * 2 + par
                    if not (first or (par and isinstance(pair, int))):
                        sp.wait_ge(packed, (blk - 1) * STEPS)
                    src = g.rows1[0:1, bass.ds(blk * R, R)]
                    sp.dma_start(row[par][:, :], src.broadcast_to([P, R])).then_inc(row_in[par], 16)
                    for k in range(STEPS):
                        if not first or k >= RING:
                            sp.wait_ge(converted, blk * STEPS + (k + 1 - RING))
                        src = adj[bass.ds(blk * R, R), k * COLS:(k + 1) * COLS]
                        sp.dma_start(ints[k % RING][:, :, :], src.rearrange("(t p) c -> p t c", p=P)
                                     ).then_inc(int_in[k % RING], 16)
                        if k >= RING:
                            store(pair, par, k - RING)
                        elif not first:
                            store(pair - (1 - par), 1 - par, k - RING + STEPS)

                over_blocks(sp, program)
                for k in range(STEPS - RING, STEPS):
                    store(BLOCKS // 2 - 1, 1, k)
                for q in range(RING):
                    sp.wait_ge(stored[q], BLOCKS * STEPS // RING * 16)

            @block.scalar
            def _(act):
                def program(pair, par, first):
                    blk = pair * 2 + par
                    act.wait_ge(row_in[par], (pair + 1) * 16)
                    for k in range(STEPS):
                        q, n = k % RING, blk * STEPS + k
                        if not first or k >= RING:
                            act.wait_ge(masks, blk * STEPS + (k + 1 - RING))
                        for t in range(J):
                            nc.scalar.activation(sgn[q][:, t * R:(t + 1) * R], row[par][:, :], ACT.Sign,
                                                 bias=g.score[:, k * J + t:k * J + t + 1])
                        if not first or k >= RING:
                            act.wait_ge(stored[q], (blk * (STEPS // RING) + k // RING) * 16)
                        act.wait_ge(turned, n + 1)
                        nc.scalar.activation(pack[q][:, :, :].rearrange("p t i -> p (t i)"), turn[:, k % 2, :], ACT.Copy,
                                             scale=-1.0).then_inc(packed, 1)

                over_blocks(act, program)

            @block.vector
            def _(dve):
                def sums_out(blk):
                    dve.wait_ge(sums_used, blk + 1)
                    for b in range(BANKS):
                        dve.wait_ge(acc_ready, blk * BANKS + (b + 1))
                        nc.vector.tensor_copy(raw[:, b, :], acc[:, b, 0:W3]).then_inc(acc_free, 1)

                def edge_signs(blk, k):
                    dve.wait_ge(packed, blk * STEPS + (k + 1))
                    nc.vector.tensor_tensor(sgn[k % RING][:, :], sgn[k % RING][:, :],
                                            pack[k % RING][:, :, :].rearrange("p t i -> p (t i)"), ALU.mult).then_inc(edges, 1)

                def split_signs(blk, k, reused=True):
                    if reused:
                        dve.wait_ge(used, blk * STEPS + (k - 1))
                    dve.wait_ge(edges, blk * STEPS + (k + 1))
                    nc.vector.tensor_scalar(mask[k % 2][1][:, :], sgn[k % RING][:, :], 0.0, None, ALU.max)
                    nc.vector.tensor_scalar(mask[k % 2][0][:, :], sgn[k % RING][:, :], -1.0, 0.0,
                                            ALU.mult, ALU.max).then_inc(masks, 1)

                def program(pair, par, first):
                    blk = pair * 2 + par
                    for k in range(STEPS):
                        q, n = k % RING, blk * STEPS + k
                        dve.wait_ge(int_in[q], (blk * (STEPS // RING) + (k // RING + 1)) * 16)
                        if not first or k >= 2:
                            dve.wait_ge(turned, blk * STEPS + (k - 1))
                        nc.vector.tensor_scalar(ones[k % 2][:, :, :], ints[q][:, :, :], 0, None,
                                                ALU.is_gt).then_inc(converted, 1)
                        if k == 3:
                            sums_out(blk)
                        if k >= 2:
                            split_signs(blk, k - 2, reused=not first or k >= 4)
                        elif not first:
                            split_signs(blk - 1, k - 2 + STEPS)
                        if k >= 1:
                            edge_signs(blk, k - 1)
                        elif not first:
                            edge_signs(blk - 1, STEPS - 1)

                over_blocks(dve, program)
                split_signs(BLOCKS - 1, STEPS - 2)
                edge_signs(BLOCKS - 1, STEPS - 1)
                split_signs(BLOCKS - 1, STEPS - 1)
                sums_out(BLOCKS)

            @block.tensor
            def _(pe):
                def multiply(blk, k):
                    pe.wait_ge(masks, blk * STEPS + (k + 1))
                    for b in range(NB):
                        if k == 0:
                            pe.wait_ge(acc_free, blk * BANKS + 2 * (b + 1))
                        for t in range(J):
                            for s in range(2):
                                at = (k * J + t) * 2 * W3 + s * W3
                                last = nc.tensor.matmul(acc[:, 2 * b + s, 0:W3],
                                                        mask[k % 2][s][:, t * R + b * P:t * R + (b + 1) * P],
                                                        g.split[:, at:at + W3], start=k == 0 and t == 0, stop=False,
                                                        skip_group_check=True)
                    last.then_inc(used, 1)
                    if k == STEPS - 1:
                        for b in range(BANKS):
                            close_bank(nc, g, acc, b).then_inc(acc_ready, 1)

                def program(pair, par, first):
                    blk = pair * 2 + par
                    for k in range(STEPS):
                        pe.wait_ge(converted, blk * STEPS + (k + 1))
                        if not first or k >= 2:
                            pe.wait_ge(packed, blk * STEPS + (k - 1))
                        for t in range(J):
                            for i in range(NB):
                                at = t * R + i * P
                                last = nc.tensor.transpose(turn[:, k % 2, at:at + P], ones[k % 2][:, i, t * P:(t + 1) * P],
                                                           g.identb[:, :])
                        last.then_inc(turned, 1)
                        if k >= 2:
                            multiply(blk, k - 2)
                        elif not first:
                            multiply(blk - 1, k - 2 + STEPS)

                for b in range(BANKS):
                    zero_bank(nc, g, acc, b, W3).then_inc(acc_ready, 1)
                over_blocks(pe, program)
                multiply(BLOCKS - 1, STEPS - 2)
                multiply(BLOCKS - 1, STEPS - 1)

            @block.gpsimd
            def _(pool):
                pool.sem_inc(sums_used, 1)
                pool.wait_ge(acc_free, BANKS)
                pool.sem_inc(sums_used, 1)
                one_head_rows(nc, pool, g, 0, NB, BLOCKS, raw, tot, res, tmp, flag, acc_free, sums_used, chain, stood)


def in_pairs(engine, count, program):
    program(0, 0, True)
    program(1, 1, False)
    with engine.Fori(1, count // 2) as pair:
        program(pair * 2, 0, False)
        program(pair * 2 + 1, 1, False)


def update_nodes(nc, sem, g, layer, x_in, out, go=None):
    before = KINDS[layer - 1] if layer else None
    kind = KINDS[layer] if layer < 4 else None
    elu = layer < 4
    tag = f"{layer}" if go is None else f"{layer}x"
    PART = 8
    PARTS = T // PART
    with ExitStack() as st:
        def sb(name, shape, dt=F32):
            return st.enter_context(nc.sbuf_tensor(f"{name}_{tag}", shape, dt))

        x = sb("x", [P, T, F])
        vals = sb("vals", [P, T * ROW_MAX])
        stats = sb("stats", [P, PART, 6])
        pair = sb("pair", [P, PART, 2])
        mv = sb("mv", [P, T, 2])
        rstd = sb("rstd", [P, T])
        x_landed, s_landed = sem("x_landed"), sem("s_landed")
        inverted, divided, low, raised, bent = sem("inverted"), sem("divided"), sem("low"), sem("raised"), sem("bent")
        x_ready, measured = sem("x_ready"), sem("measured")
        stood = sem("stood")
        x_src = x_in if layer < 2 else g.nodes
        with ExitStack() as st1:
            frac = [st1.enter_context(nc.sbuf_tensor(f"frac{b}_{tag}", [P, PART, F], F32)) for b in range(2)]
            expm = [st1.enter_context(nc.sbuf_tensor(f"expm{b}_{tag}", [P, PART * F], F32)) for b in range(2)]
            rden = [st1.enter_context(nc.sbuf_tensor(f"rden{b}_{tag}", [P, PART * 4], F32)) for b in range(2)]
            with nc.Block() as plain:
                block = guarded(plain, go)

                @block.sync
                def _(sp):
                    HALVES = PARTS // 4 if layer == 4 else PARTS
                    with sp.Fori(0, PARTS // HALVES) as head:
                        with sp.Fori(0, HALVES) as half:
                            p = head * HALVES + half
                            rows = x_src[bass.ds(p * (PART * P), PART * P), :].rearrange("(t p) f -> p t f", p=P)
                            sp.dma_start(x[:, bass.ds(p * PART, PART), :], rows).then_inc(x_landed, 16)
                            if before:
                                row = before.heads * before.width
                                if layer < 4:
                                    src = g.sums[layer - 1][bass.ds(p * PART, PART)].rearrange("t p w -> p t w")
                                else:
                                    src = g.sums[3][bass.ds(head, 1), bass.ds(half * (PART * P * 4), PART * P * 4), :]
                                    src = src.rearrange("a (t p i) w -> p (a t) (i w)", p=P, i=4)
                                dst = vals[:, bass.ds(p * (PART * row), PART * row)]
                                sp.dma_start(dst.rearrange("p (t w) -> p t w", t=PART), src).then_inc(s_landed, 16)
                                sp.wait_ge(s_landed, (p + 1) * 16)
                            sp.wait_ge(x_landed, (p + 1) * 16)
                            sp.sem_inc(stood, 1)

                @block.gpsimd
                def _(pool):
                    if before:
                        dst = out if layer == 4 else g.nodes
                        with pool.Fori(0, PARTS) as p:
                            pool.wait_ge(x_ready, p + 1)
                            rows = dst[bass.ds(p * (PART * P), PART * P), :].rearrange("(t p) f -> p t f", p=P)
                            pool.dma_start(rows, x[:, bass.ds(p * PART, PART), :]).then_inc(g.pool_stored, 16)
                        g.pool_stores += 16 * PARTS
                        pool.wait_ge(g.pool_stored, g.pool_stores)

                @block.scalar
                def _(act):
                    if before and elu:
                        with act.Fori(0, PARTS // 2) as pp:
                            for b in range(2):
                                act.wait_ge(low, pp * 2 + (b + 1))
                                nc.scalar.activation(expm[b][:, :], expm[b][:, :], ACT.Exp).then_inc(raised, 1)

                @block.vector
                def _(dve):
                    H, W = (before.heads, before.width) if before else (0, 0)

                    def sums(p):
                        return vals[:, bass.ds(p * (PART * H * W), PART * H * W)].rearrange("p (u w) -> p u w", w=W)

                    def shares(b):
                        return frac[b][:, :, :].rearrange("p t (h d) -> p (t h) d", h=H)

                    def flat(b):
                        return frac[b][:, :, :].rearrange("p t f -> p (t f)")

                    def invert(p, b):
                        dve.wait_ge(s_landed, (p + 1) * 16)
                        nc.vector.reciprocal(rden[b][:, 0:PART * H], sums(p)[:, :, W - 1]).then_inc(inverted, 1)

                    def divide(p, b):
                        dve.wait_ge(inverted, p + 1)
                        r = rden[b][:, 0:PART * H].unsqueeze(2).broadcast_to([P, PART * H, W - 1])
                        nc.vector.tensor_tensor(shares(b), sums(p)[:, :, 0:W - 1], r, ALU.mult).then_inc(divided, 1)

                    def lower(p, b):
                        dve.wait_ge(divided, p + 1)
                        nc.vector.tensor_scalar(expm[b][:, :], flat(b), 0.0, None, ALU.min).then_inc(low, 1)

                    def bend(p, b):
                        dve.wait_ge(raised, p + 1)
                        nc.vector.scalar_tensor_tensor(expm[b][:, :], flat(b), 0.0, expm[b][:, :],
                                                       ALU.max, ALU.add).then_inc(bent, 1)

                    def add(p, b):
                        dve.wait_ge(x_landed, (p + 1) * 16)
                        xp = x[:, bass.ds(p * PART, PART), :]
                        if elu:
                            dve.wait_ge(bent, p + 1)
                            nc.vector.scalar_tensor_tensor(xp, expm[b][:, :].rearrange("p (t f) -> p t f", f=F), -1.0,
                                                           xp, ALU.add, ALU.add).then_inc(x_ready, 1)
                        else:
                            dve.wait_ge(divided, p + 1)
                            nc.vector.tensor_tensor(xp, frac[b][:, :, :], xp, ALU.add).then_inc(x_ready, 1)

                    def measure(p):
                        if before:
                            dve.wait_ge(x_ready, p + 1)
                        else:
                            dve.wait_ge(x_landed, (p + 1) * 16)
                        dve.sem_inc(stood, 1)
                        for t in range(PART):
                            last = nc.vector.bn_stats(stats[:, t, :], x[:, bass.ds(p * PART + t, 1), :]
                                                      .rearrange("p a f -> p (a f)"))
                        last.then_inc(measured, 1)
                        dve.wait_ge(measured, 3 * p + 1)
                        dve.sem_inc(stood, 1)
                        for t in range(PART):
                            last = nc.vector.bn_aggr(pair[:, t, :], stats[:, t, :])
                        last.then_inc(measured, 1)
                        dve.wait_ge(measured, 3 * p + 2)
                        nc.vector.tensor_copy(mv[:, bass.ds(p * PART, PART), :], pair[:, :, :]).then_inc(measured, 1)
                        dve.wait_ge(measured, 3 * p + 3)

                    def part(p, b, first):
                        if not before:
                            measure(p)
                            return
                        invert(p, b)
                        if elu and not first:
                            bend(p - 1, 1 - b)
                        divide(p, b)
                        if not first:
                            add(p - 1, 1 - b)
                        if elu:
                            lower(p, b)
                        if kind and not first:
                            measure(p - 1)

                    in_pairs(dve, PARTS, part)
                    if before:
                        if elu:
                            bend(PARTS - 1, 1)
                        add(PARTS - 1, 1)
                        if kind:
                            measure(PARTS - 1)
        if not kind:
            return
        H, W = kind.heads, kind.width
        ROW = H * W
        CH = 4
        CHUNKS = T // CH
        cols = F + 2 * H
        scol = sb("scol", [P, T, 2 * H])
        with ExitStack() as st2:
            hn = [st2.enter_context(nc.sbuf_tensor(f"hn{b}_{tag}", [P, CH, F], F32)) for b in range(2)]
            ht = [st2.enter_context(nc.sbuf_tensor(f"ht{b}_{tag}", [P, CH * P], F32)) for b in range(2)]
            srow = [st2.enter_context(nc.sbuf_tensor(f"srow{b}_{tag}", [H, CH * P], F32)) for b in range(2)]
            pt = [st2.enter_context(nc.psum_tensor(f"pt{b}_{tag}", [P, CH * P], F32)) for b in range(2)]
            pv = [st2.enter_context(nc.psum_tensor(f"pv{b}_{tag}", [P, 2, BANK], F32)) for b in range(2)]
            ps = [st2.enter_context(nc.psum_tensor(f"ps{b}_{tag}", [P, BANK], F32)) for b in range(2)]
            rooted, inverse = sem("rooted"), sem("inverse")
            h_ready, turned, ht_ready, projected = sem("h_ready"), sem("turned"), sem("ht_ready"), sem("projected")
            v_copied, row_made, row_ready = sem("v_copied"), sem("row_made"), sem("row_ready")
            row_out, row_free, ones_set = sem("row_out"), sem("row_free"), sem("ones_set")
            with nc.Block() as plain:
                block = guarded(plain, go)

                @block.gpsimd
                def _(pool):
                    u = vals[:, 0:T * ROW].rearrange("p (u w) -> p u w", w=W)
                    nc.gpsimd.memset(u[:, :, W - 1], 1.0).then_inc(ones_set, 1)

                @block.sync
                def _(sp):
                    sp.sem_inc(row_free, 2)
                    with sp.Fori(0, CHUNKS // 2) as cc:
                        for b in range(2):
                            c = cc * 2 + b
                            sp.wait_ge(row_ready, c + 1)
                            sp.dma_start(g.rows1[0:H, bass.ds(c * (CH * P), CH * P)], srow[b][:, :]).then_inc(row_out, 16)
                            sp.wait_ge(row_out, (c + 1) * 16)
                            sp.sem_inc(row_free, 1)

                @block.vector
                def _(dve):
                    nc.vector.tensor_scalar(rstd[:, :], mv[:, :, 1], EPS, None, ALU.add).then_inc(rooted, 1)
                    dve.wait_ge(rooted, 2)
                    nc.vector.reciprocal(rstd[:, :], rstd[:, :]).then_inc(inverse, 1)
                    dve.wait_ge(inverse, 1)

                    def score_row(c, b):
                        dve.wait_ge(projected, c + 1)
                        dve.wait_ge(row_free, c + 1)
                        nc.vector.tensor_scalar(srow[b][:, :], ps[b][0:H, :], TINY, None, ALU.add).then_inc(row_made, 1)
                        dve.wait_ge(row_made, c + 1)
                        bits = srow[b][:, :].bitcast(I32)
                        nc.vector.tensor_scalar(bits, bits, 1, None, ALU.bitwise_or).then_inc(row_ready, 1)

                    def normalise(c, b, first):
                        dve.wait_ge(turned, c + 1)
                        for t in range(CH):
                            tile = bass.ds(c * CH + t, 1)
                            last = nc.vector.tensor_scalar(
                                hn[b][:, t, :], x[:, tile, :].rearrange("p a f -> p (a f)"),
                                mv[:, tile, 0:1].rearrange("p a f -> p (a f)"), rstd[:, tile],
                                ALU.subtract, ALU.mult)
                        last.then_inc(h_ready, 1)
                        if not isinstance(c, int) or c >= 2:
                            score_row(c - 2, b)

                    in_pairs(dve, CHUNKS, normalise)
                    score_row(CHUNKS - 2, 0)
                    score_row(CHUNKS - 1, 1)

                @block.tensor
                def _(pe):
                    pe.sem_inc(turned, 2)

                    def project(c, b):
                        pe.wait_ge(ht_ready, c + 3)
                        if not isinstance(c, int) or c >= 2:
                            pe.wait_ge(v_copied, c - 1)
                            pe.wait_ge(row_made, c - 1)
                        for t in range(CH):
                            nc.tensor.matmul(pv[b][:, t // 2, (t % 2) * cols:(t % 2 + 1) * cols],
                                             ht[b][:, t * P:(t + 1) * P], g.waug[:, layer, 0:cols],
                                             start=True, stop=True)
                        nc.tensor.matmul(ps[b][0:H, :], g.waug[:, layer, F:F + H], ht[b][:, :],
                                         start=True, stop=True).then_inc(projected, 1)

                    def transpose(c, b, first):
                        pe.wait_ge(h_ready, c + 1)
                        pe.wait_ge(ht_ready, c + 1)
                        for t in range(CH):
                            last = nc.tensor.transpose(pt[b][:, t * P:(t + 1) * P], hn[b][:, t, :], g.identf[:, :])
                        last.then_inc(turned, 1)
                        if not first:
                            project(c - 1, 1 - b)

                    in_pairs(pe, CHUNKS, transpose)
                    project(CHUNKS - 1, 1)

                @block.scalar
                def _(act):
                    act.wait_ge(rooted, 1)
                    nc.scalar.activation(rstd[:, :], rstd[:, :], ACT.Sqrt).then_inc(rooted, 1)
                    act.sem_inc(ht_ready, 2)

                    def copy_values(c, b):
                        act.wait_ge(projected, c + 1)
                        for k in range(2):
                            src = pv[b][:, k, 0:2 * cols].rearrange("p (t c) -> p t c", c=cols)[:, :, F:cols]
                            nc.scalar.activation(scol[:, bass.ds(c * CH + 2 * k, 2), :], src, ACT.Copy)
                            dst = vals[:, bass.ds((c * CH + 2 * k) * ROW, 2 * ROW)]
                            dst = dst.rearrange("p (t h w) -> p t h w", t=2, h=H)[:, :, :, 0:W - 1]
                            src = pv[b][:, k, 0:2 * cols].rearrange("p (t c) -> p t c", c=cols)[:, :, 0:F]
                            src = src.rearrange("p t (h d) -> p t h d", h=H)
                            last = nc.scalar.activation(dst, src, ACT.Copy)
                        last.then_inc(v_copied, 1)

                    def rectify(c, b, first):
                        act.wait_ge(turned, c + 3)
                        nc.scalar.activation(ht[b][:, :], pt[b][:, :], ACT.Relu).then_inc(ht_ready, 1)
                        if not first:
                            copy_values(c - 1, 1 - b)

                    in_pairs(act, CHUNKS, rectify)
                    copy_values(CHUNKS - 1, 1)

        if go is not None:
            store_for_exact(nc, sem, g, kind, scol, vals, go)
            return

        with ExitStack() as st3:
            def sb3(name, shape, dt=F32):
                return st3.enter_context(nc.sbuf_tensor(f"{name}_{tag}", shape, dt))

            ends, most = sb3("ends", [P, 2 * H]), sb3("most", [P, 2 * H])
            tlow, thigh, u = sb3("tlow", [P, T, H]), sb3("thigh", [P, T, H]), sb3("u", [P, T, H])
            col = [sb3("ca", [P, T, H]), sb3("cb", [P, T, H])]
            UT = 4
            whole = [sb3(f"whole{b}", [P, UT * ROW]) for b in range(2)]
            rest = [sb3(f"rest{b}", [P, UT * ROW]) for b in range(2)]
            ptot = st3.enter_context(nc.psum_tensor(f"ptot_{tag}", [P, BANK], F32))
            UNITS = T // UT * 2
            ends_ready, most_ready, spread, exps = sem("ends_ready"), sem("most_ready"), sem("spread"), sem("exps")
            totalled, ranged = sem("totalled"), sem("ranged")
            wholes, highs, rests, mids, lows = sem("wholes"), sem("highs"), sem("rests"), sem("mids"), sem("lows")
            pieces = g.split[:, 0:T * 2 * PIECES * ROW].rearrange("p (t c q w) -> p t c q w", t=T, q=PIECES, w=W)

            def piece(cc, side, q):
                v = pieces[:, bass.ds(cc * UT, UT), :, q, :]
                if H == 1:
                    return v[:, :, side:side + 1, :]
                v = v.rearrange("p t (g c) w -> p (t g) c w", c=4)
                return v[:, :, 1:3, :] if side == 0 else v[:, :, 0:4:3, :]

            def by_side(engine, program):
                program(0, 0, True)
                program(0, 1, False)
                with engine.Fori(1, T // UT) as cc:
                    program(cc, 0, False)
                    program(cc, 1, False)

            def unit(buf):
                return buf[:, :].rearrange("p (t h w) -> p t h w", h=min(H, 2), w=W)

            with nc.Block() as plain:
                block = guarded(plain, go)

                @block.gpsimd
                def _(pool):
                    pool.wait_ge(ends_ready, 2)
                    nc.gpsimd.partition_all_reduce(most[:, :], ends[:, :], P, RMAX).then_inc(most_ready, 1)
                    pool.wait_ge(exps, 2)
                    with pool.Fori(0, T // UT) as cc:
                        for side in range(2):
                            pool.wait_ge(rests, cc * 2 + side + 1)
                            v = vals[:, bass.ds(cc * (UT * ROW), UT * ROW)].rearrange("p (t h w) -> p t h w", t=UT, h=H)
                            c = col[side][:, bass.ds(cc * UT, UT), :].unsqueeze(3).broadcast_to([P, UT, H, W])
                            dst = whole[side][:, :].rearrange("p (t h w) -> p t h w", t=UT, h=H)
                            nc.gpsimd.tensor_tensor(dst, v, c, ALU.mult).then_inc(wholes, 1)

                @block.tensor
                def _(pe):
                    nc.tensor.matmul(ptot[:, 0:ROW], g.onesf[:, :], vals[:, 0:ROW], start=True, stop=False)
                    with pe.Fori(1, T - 1) as t:
                        nc.tensor.matmul(ptot[:, 0:ROW], g.onesf[:, :], vals[:, bass.ds(t * ROW, ROW)],
                                         start=False, stop=False)
                    nc.tensor.matmul(ptot[:, 0:ROW], g.onesf[:, :], vals[:, (T - 1) * ROW:T * ROW],
                                     start=False, stop=True).then_inc(totalled, 1)

                @block.scalar
                def _(act):
                    act.wait_ge(spread, 2)
                    nc.scalar.activation(col[0][:, :, :], u[:, :, :], ACT.Exp).then_inc(exps, 1)
                    nc.scalar.activation(col[1][:, :, :], u[:, :, :], ACT.Exp, scale=ALPHA).then_inc(exps, 1)
                    act.wait_ge(spread, 4)
                    nc.scalar.activation(g.ra[:, 0:T * H], tlow[:, :, :].rearrange("p t h -> p (t h)"), ACT.Exp,
                                         scale=1 - ALPHA).then_inc(exps, 1)
                    nc.scalar.activation(g.rb[:, 0:T * H], thigh[:, :, :].rearrange("p t h -> p (t h)"), ACT.Exp,
                                         scale=ALPHA - 1).then_inc(exps, 1)

                    def middle(cc, side):
                        act.wait_ge(rests, cc * 2 + (side + 3))
                        nc.scalar.activation(piece(cc, side, 1), unit(rest[side]), ACT.Copy).then_inc(mids, 1)

                    def high(cc, side, first):
                        act.wait_ge(wholes, cc * 2 + (side + 1))
                        nc.scalar.activation(piece(cc, side, 0), unit(whole[side]), ACT.Copy).then_inc(highs, 1)
                        if not first:
                            middle(cc - (1 - side), 1 - side)

                    by_side(act, high)
                    middle(T // UT - 1, 1)

                @block.vector
                def _(dve):
                    dve.sem_inc(rests, 2)
                    dve.sem_inc(lows, 2)
                    s2 = scol[:, :, H:2 * H]
                    nc.vector.tensor_reduce(ends[:, 0:H], s2.rearrange("p t h -> p h t"), AX.X, ALU.max).then_inc(ends_ready, 1)
                    nc.vector.tensor_reduce(ends[:, H:2 * H], s2.rearrange("p t h -> p h t"), AX.X, ALU.min,
                                            negate=True).then_inc(ends_ready, 1)
                    dve.wait_ge(most_ready, 1)
                    nc.vector.tensor_tensor(ends[:, 0:H], most[:, 0:H], most[:, H:2 * H], ALU.add).then_inc(ranged, 1)
                    dve.wait_ge(ranged, 1)
                    nc.vector.tensor_reduce(ends[:, H:H + 1], ends[:, 0:H], AX.X, ALU.max).then_inc(ranged, 1)
                    dve.wait_ge(ranged, 2)
                    nc.vector.tensor_tensor(g.widest[:, :], g.widest[:, :], ends[:, H:H + 1], ALU.max)
                    top = most[:, 0:H].unsqueeze(1).broadcast_to([P, T, H])
                    nc.vector.tensor_tensor(u[:, :, :], s2, top, ALU.subtract).then_inc(spread, 1)
                    nc.vector.tensor_tensor(thigh[:, :, :], scol[:, :, 0:H], top, ALU.add).then_inc(spread, 1)
                    dve.wait_ge(spread, 2)
                    nc.vector.tensor_scalar(tlow[:, :, :], thigh[:, :, :], 0.0, None, ALU.min).then_inc(spread, 1)
                    dve.wait_ge(spread, 3)
                    nc.vector.tensor_scalar(thigh[:, :, :], thigh[:, :, :], 0.0, None, ALU.max).then_inc(spread, 1)
                    nc.vector.tensor_scalar(g.score[:, 0:T * H].rearrange("p (t h) -> p t h", h=H).bitcast(I32),
                                            s2.bitcast(I32), -2, None, ALU.bitwise_and).then_inc(ends_ready, 1)
                    def low(cc, side):
                        dve.wait_ge(mids, cc * 2 + (side + 1))
                        nc.vector.tensor_tensor(piece(cc, side, 2), unit(rest[side]), piece(cc, side, 1),
                                                ALU.subtract).then_inc(lows, 1)

                    def remainder(cc, side, first):
                        dve.wait_ge(highs, cc * 2 + (side + 1))
                        dve.wait_ge(lows, cc * 2 + (side + 1))
                        nc.vector.tensor_tensor(unit(rest[side]), unit(whole[side]), piece(cc, side, 0),
                                                ALU.subtract).then_inc(rests, 1)
                        if not first:
                            low(cc - (1 - side), 1 - side)

                    by_side(dve, remainder)
                    dve.wait_ge(rests, UNITS + 2)
                    low(T // UT - 1, 1)
                    dve.wait_ge(totalled, 1)
                    nc.vector.tensor_copy(g.colsum[:, 0:ROW], ptot[:, 0:ROW]).then_inc(ends_ready, 1)


def store_for_exact(nc, sem, g, kind, scol, vals, go):
    H, ROW = kind.heads, kind.heads * kind.width
    saved = sem("saved")
    with nc.Block() as plain:
        block = guarded(plain, go)

        @block.sync
        def _(sp):
            for k in range(2):
                for h in range(H):
                    sp.dma_start(g.scores[k, h].rearrange("t p -> p t"), scol[:, :, k * H + h]).then_inc(saved, 16)
            sp.dma_start(g.values[:, 0:T * ROW], vals[:, 0:T * ROW]).then_inc(saved, 16)
            sp.wait_ge(saved, 16 * (2 * H + 1))


def decide(nc, sem, g):
    decided = sem("decided")
    with nc.Block() as block:

        @block.vector
        def _(dve):
            nc.vector.tensor_scalar(g.exact[:, :], g.widest[:, :], WIDEST, None, ALU.is_gt).then_inc(decided, 1)
            dve.wait_ge(decided, 1)


def attend_exact(nc, sem, g, layer, adj, go):
    kind = KINDS[layer]
    H, W = kind.heads, kind.width
    ROW = H * W
    GROUP = 4
    GROUPS = T // GROUP
    LINKS = 6
    adj_in, vals_in, row_in, row_used, shifted = sem("adj_in"), sem("vals_in"), sem("row_in"), sem("row_used"), sem("shifted")
    raised, turned, copied, added = sem("raised"), sem("turned"), sem("copied"), sem("added")
    summed, held, sums_out, chain, stood = sem("summed"), sem("held"), sem("sums_out"), sem("chain"), sem("stood")
    res_free = sem("res_free")
    with ExitStack() as st:
        def sb(name, shape, dt=F32):
            return st.enter_context(nc.sbuf_tensor(f"x{name}_{layer}", shape, dt))

        ints = sb("ints", [P, N], I32)
        edge = sb("edge", [P, N])
        row = sb("row", [P, N])
        e = sb("e", [P, N])
        s1 = sb("s1", [P, H, T])
        vals = sb("vals", [P, T * ROW])
        top, ntop = sb("top", [P, 1]), sb("ntop", [P, 1])
        pt = [sb(f"pt{b}", [P, GROUP * P]) for b in range(2)]
        res = sb("res", [P, W])
        turn = [st.enter_context(nc.psum_tensor(f"xturn{b}_{layer}", [P, GROUP * P], F32)) for b in range(2)]
        acc = st.enter_context(nc.psum_tensor(f"xacc_{layer}", [P, BANK], F32))
        with nc.Block() as plain:
            block = guarded(plain, go)

            @block.sync
            def _(sp):
                sp.sem_inc(res_free, 1)
                sp.dma_start(vals[:, :], g.values[:, 0:T * ROW]).then_inc(vals_in, 16)
                for h in range(H):
                    sp.dma_start(s1[:, h, :], g.scores[0, h].rearrange("t p -> p t")).then_inc(vals_in, 16)
                for h in range(H):
                    if h:
                        sp.wait_ge(row_used, h * T)
                    src = g.scores[1, h].rearrange("t p -> (t p)").unsqueeze(0).broadcast_to([P, N])
                    sp.dma_start(row[:, :], src).then_inc(row_in, 16)
                    with sp.Fori(0, T) as it:
                        n = it + h * T
                        sp.wait_ge(chain, n * LINKS + 1)
                        sp.dma_start(ints[:, :], adj[bass.ds(it * P, P), :]).then_inc(adj_in, 16)
                        sp.wait_ge(held, n + 1)
                        if layer < 3:
                            dst = g.sums[layer][bass.ds(it, 1), :, h * W:(h + 1) * W].rearrange("a p w -> (a p) w")
                        else:
                            dst = g.sums[layer][h, bass.ds(it * P, P), :]
                        sp.dma_start(dst, res[:, :]).then_inc(sums_out, 16)
                        sp.wait_ge(sums_out, (n + 1) * 16)
                        sp.sem_inc(res_free, 1)

            @block.vector
            def _(dve):
                dve.sem_inc(chain, LINKS)
                dve.wait_ge(vals_in, 16 * (1 + H))
                for h in range(H):
                    dve.wait_ge(row_in, 16 * (h + 1))
                    with dve.Fori(0, T) as it:
                        n = it + h * T
                        made = [0]

                        def link(ins):
                            made[0] += 1
                            ins.then_inc(chain, 1)
                            dve.wait_ge(chain, (n + 1) * LINKS + made[0])

                        dve.wait_ge(adj_in, (n + 1) * 16)
                        link(nc.vector.tensor_scalar(edge[:, :], ints[:, :], 0, None, ALU.is_gt))
                        dve.wait_ge(summed, n + 1)
                        nc.vector.tensor_scalar(e[:, :], row[:, :], s1[:, h, bass.ds(it, 1)], None,
                                                ALU.add).then_inc(row_used, 1)
                        dve.wait_ge(row_used, n + 1)
                        link(nc.vector.scalar_tensor_tensor(e[:, :], e[:, :], ALPHA, e[:, :], ALU.mult, ALU.max))
                        link(nc.vector.tensor_tensor(e[:, :], e[:, :], edge[:, :], ALU.mult))
                        link(nc.vector.tensor_scalar(edge[:, :], edge[:, :], -1.0, -NEG_INF, ALU.add, ALU.mult))
                        link(nc.vector.tensor_tensor(e[:, :], e[:, :], edge[:, :], ALU.add))
                        link(nc.vector.tensor_reduce(top[:, :], e[:, :], AX.X, ALU.max))
                        nc.vector.tensor_scalar(ntop[:, :], top[:, :], -1.0, None, ALU.mult).then_inc(shifted, 1)

            @block.scalar
            def _(act):
                with act.Fori(0, H * T) as n:
                    act.wait_ge(shifted, n + 1)
                    nc.scalar.activation(e[:, :], e[:, :], ACT.Exp, bias=ntop[:, :]).then_inc(raised, 1)
                    with act.Fori(0, GROUPS // 2) as j:
                        for b in range(2):
                            k = n * GROUPS + j * 2 + b
                            act.wait_ge(turned, k + 1)
                            act.wait_ge(added, k + 1)
                            nc.scalar.activation(pt[b][:, :], turn[b][:, :], ACT.Copy).then_inc(copied, 1)
                    act.wait_ge(summed, n + 2)
                    act.wait_ge(res_free, n + 1)
                    nc.scalar.activation(res[:, :], acc[:, 0:W], ACT.Copy).then_inc(held, 1)

            @block.tensor
            def _(pe):
                pe.sem_inc(summed, 1)
                pe.sem_inc(added, 2)
                pe.wait_ge(vals_in, 16 * (1 + H))
                with pe.Fori(0, H) as h:
                    with pe.Fori(0, T) as it:
                        n = it + h * T
                        pe.wait_ge(raised, n + 1)
                        nc.tensor.matmul(acc[:, 0:2], g.zeros[:, :], g.zeros[:, 0:2], start=True, stop=False,
                                         skip_group_check=True)
                        for j in range(GROUPS):
                            for t in range(GROUP):
                                at = (j * GROUP + t) * P
                                last = nc.tensor.transpose(turn[j % 2][:, t * P:(t + 1) * P], e[:, at:at + P],
                                                           g.identf[:, :])
                            last.then_inc(turned, 1)
                            pe.wait_ge(copied, n * GROUPS + (j + 1))
                            for t in range(GROUP):
                                rhs = vals[:, bass.ds(h * W + (j * GROUP + t) * ROW, W)]
                                last = nc.tensor.matmul(acc[:, 0:W], pt[j % 2][:, t * P:(t + 1) * P], rhs,
                                                        start=False, stop=False, skip_group_check=True)
                            last.then_inc(added, 1)
                        nc.tensor.matmul(acc[:, 0:2], g.zeros[:, :], g.zeros[:, 0:2], start=False, stop=True,
                                         skip_group_check=True).then_inc(summed, 1)


def attend_one(nc, sem, g, layer):
    W = F + 1
    W3 = PIECES * W
    R, J, LT = 512, 4, 8
    NB = R // P
    BLOCKS = N // R
    STEPS_LOAD = LT // J
    LOOPS = T // (2 * LT)
    STEPS_ITER = 2 * STEPS_LOAD
    STEPS = LOOPS * STEPS_ITER
    SIGNS = 4
    WIDE = J * R
    adj_in = [sem("adj_in0"), sem("adj_in1")]
    row_in = [sem("row_in0"), sem("row_in1")]
    signs, edges, masks, used = sem("signs"), sem("edges"), sem("masks"), sem("used")
    acc_ready, acc_free, sums_used, chain = sem("acc_ready"), sem("acc_free"), sem("sums_used"), sem("chain")
    stood = sem("stood")
    with ExitStack() as st:
        def sb(name, shape, dt=F32):
            return st.enter_context(nc.sbuf_tensor(f"{name}_{layer}", shape, dt))

        adj = [sb(f"adj{q}", [P, LT, IBLK], BF16) for q in range(2)]
        row = [sb(f"row{q}", [P, R]) for q in range(2)]
        sgn = [sb(f"sgn{q}", [P, WIDE], BF16) for q in range(SIGNS)]
        mask = [[sb(f"mask{q}{s}", [P, WIDE], BF16) for s in range(2)] for q in range(2)]
        acc = st.enter_context(nc.psum_tensor(f"acc_{layer}", [P, 8, BANK], F32))
        raw = sb("raw", [P, 8, W3])
        tot = sb("tot", [P, NB * 2, W])
        res, tmp = sb("res", [P, NB, W]), sb("tmp", [P, NB, W])
        flag = sb("flag", [P, NB])
        with nc.Block() as block:

            @block.sync
            def _(sp):
                with sp.Fori(0, BLOCKS // 2) as bb:
                    for par in range(2):
                        blk = bb * 2 + par
                        sp.wait_ge(signs, (blk + 1) * STEPS)
                        src = g.rows1[0:1, bass.ds(blk * R, R)]
                        sp.dma_start(row[par][:, :], src.broadcast_to([P, R])).then_inc(row_in[par], 16)
                        with sp.Fori(0, LOOPS) as j:
                            for q in range(2):
                                load = (blk * LOOPS + j) * 2 + q
                                sp.wait_ge(edges, (load + 1) * STEPS_LOAD)
                                src = g.adj_t[bass.ds(blk, 1), :, bass.ds((j * 2 + q) * LT, LT), :]
                                sp.dma_start(adj[q][:, :, :], src.rearrange("s p t i -> p (s t) i")).then_inc(adj_in[q], 16)

            @block.scalar
            def _(act):
                act.sem_inc(signs, 2 * STEPS)
                with act.Fori(0, BLOCKS // 2) as bb:
                    for par in range(2):
                        blk = bb * 2 + par
                        act.wait_ge(row_in[par], (bb + 1) * 16)
                        with act.Fori(0, LOOPS) as j:
                            for k in range(STEPS_ITER):
                                n = (blk * LOOPS + j) * STEPS_ITER + k
                                act.wait_ge(masks, n + 1)
                                for t in range(J):
                                    col = (j * STEPS_ITER + k) * J + t
                                    last = nc.scalar.activation(sgn[k % SIGNS][:, t * R:(t + 1) * R], row[par][:, :],
                                                                ACT.Sign, bias=g.score[:, bass.ds(col, 1)])
                                last.then_inc(signs, 1)

            @block.vector
            def _(dve):
                dve.sem_inc(edges, 2 * STEPS_LOAD)
                dve.sem_inc(masks, SIGNS)

                def split_signs(it, k):
                    n = it * STEPS_ITER + k
                    dve.wait_ge(used, n + 1)
                    dve.wait_ge(edges, n + (1 + 2 * STEPS_LOAD))
                    nc.vector.tensor_scalar(mask[k % 2][1][:, :], sgn[k % SIGNS][:, :], 0.0, None, ALU.max)
                    nc.vector.tensor_scalar(mask[k % 2][0][:, :], sgn[k % SIGNS][:, :], -1.0, 0.0,
                                            ALU.mult, ALU.max).then_inc(masks, 1)

                def steps(it, evacuate=None):
                    for k in range(STEPS_ITER):
                        n = it * STEPS_ITER + k
                        q, kk = k // STEPS_LOAD, k % STEPS_LOAD
                        if kk == 0:
                            dve.wait_ge(adj_in[q], (it + 1) * 16)
                        dve.wait_ge(signs, n + (1 + 2 * STEPS))
                        s = sgn[k % SIGNS][:, :]
                        a = adj[q][:, kk * J:(kk + 1) * J, :].rearrange("p t i -> p (t i)")
                        nc.vector.tensor_tensor(s, s, a, ALU.mult).then_inc(edges, 1)
                        if k:
                            split_signs(it, k - 1)
                        if k == 2 and evacuate:
                            evacuate()
                    split_signs(it, STEPS_ITER - 1)

                def sums_out(blk):
                    dve.wait_ge(sums_used, blk + 1)
                    for b in range(8):
                        dve.wait_ge(acc_ready, blk * 8 + (b + 1))
                        nc.vector.tensor_copy(raw[:, b, :], acc[:, b, 0:W3]).then_inc(acc_free, 1)

                with dve.Fori(0, BLOCKS) as blk:
                    steps(blk * LOOPS, lambda: sums_out(blk))
                    with dve.Fori(1, LOOPS) as j:
                        steps(blk * LOOPS + j)
                sums_out(BLOCKS)

            @block.tensor
            def _(pe):
                pe.sem_inc(used, 2)
                for b in range(8):
                    zero_bank(nc, g, acc, b, W3).then_inc(acc_ready, 1)

                def add(k, tile, t, b, first):
                    for s in range(2):
                        rhs = g.split[:, bass.ds((tile + t) * (2 * W3) + s * W3, W3)]
                        last = nc.tensor.matmul(acc[:, 2 * b + s, 0:W3], mask[k % 2][s][:, t * R + b * P:t * R + (b + 1) * P],
                                                rhs, start=first, stop=False, skip_group_check=True)
                    return last

                with pe.Fori(0, BLOCKS) as blk:
                    def steps(j, opening=False):
                        for k in range(STEPS_ITER):
                            n = (blk * LOOPS + j) * STEPS_ITER + k
                            tile = (j * STEPS_ITER + k) * J
                            pe.wait_ge(masks, n + (1 + SIGNS))
                            for b in range(NB):
                                first = opening and k == 0
                                if first:
                                    pe.wait_ge(acc_free, blk * 8 + (2 * b + 2))
                                for t in range(J):
                                    last = add(k, tile, t, b, first and t == 0)
                            last.then_inc(used, 1)

                    steps(0, opening=True)
                    with pe.Fori(1, LOOPS) as j:
                        steps(j)
                    for b in range(8):
                        close_bank(nc, g, acc, b).then_inc(acc_ready, 1)

            @block.gpsimd
            def _(pool):
                pool.sem_inc(sums_used, 1)
                pool.wait_ge(acc_free, 8)
                pool.sem_inc(sums_used, 1)
                one_head_rows(nc, pool, g, layer, NB, BLOCKS, raw, tot, res, tmp, flag, acc_free, sums_used, chain, stood)


def one_head_rows(nc, pool, g, layer, NB, BLOCKS, raw, tot, res, tmp, flag, acc_free, sums_used, chain, stood):
    W = F + 1
    LINKS = 7
    before = g.pool_stores
    g.pool_stores += 16 * BLOCKS
    with pool.Fori(0, BLOCKS) as blk:
        made = [0]

        def link(ins):
            made[0] += 1
            ins.then_inc(chain, 1)
            pool.wait_ge(chain, blk * LINKS + made[0])

        def factor(v):
            return v[:, bass.ds(blk * NB, NB)].unsqueeze(2).broadcast_to([P, NB, W])

        pool.wait_ge(acc_free, blk * (2 * NB) + 4 * NB)
        r = raw[:, :, :].rearrange("p b (q w) -> p b q w", w=W)
        link(nc.gpsimd.tensor_tensor(tot[:, :, :], r[:, :, 0, :], r[:, :, 1, :], ALU.add))
        nc.gpsimd.tensor_tensor(tot[:, :, :], tot[:, :, :], r[:, :, 2, :], ALU.add).then_inc(sums_used, 1)
        pool.wait_ge(sums_used, blk + 3)
        two = tot[:, :, :].rearrange("p (u s) w -> p u s w", s=2)
        link(nc.gpsimd.tensor_tensor(res[:, :, :], two[:, :, 0, :], factor(g.ra), ALU.mult))
        link(nc.gpsimd.tensor_tensor(tmp[:, :, :], two[:, :, 1, :], factor(g.rb), ALU.mult))
        link(nc.gpsimd.tensor_tensor(res[:, :, :], res[:, :, :], tmp[:, :, :], ALU.add))
        pool.sem_inc(stood, 1)
        link(nc.gpsimd.tensor_scalar(flag[:, :], res[:, :, W - 1], 0.0, None, ALU.is_equal))
        link(nc.gpsimd.tensor_tensor(tmp[:, :, :], flag[:, :].unsqueeze(2).broadcast_to([P, NB, W]),
                                     g.colsum[:, 0:W].unsqueeze(1).broadcast_to([P, NB, W]), ALU.mult))
        link(nc.gpsimd.tensor_tensor(res[:, :, :], res[:, :, :], tmp[:, :, :], ALU.add))
        dst = g.sums[layer][bass.ds(blk * NB, NB)]
        pool.dma_start(dst.rearrange("b p w -> p b w"), res[:, :, :]).then_inc(g.pool_stored, 16)
        pool.wait_ge(g.pool_stored, (blk + 1) * 16 + before)
        pool.sem_inc(stood, 1)


def zero_bank(nc, g, acc, b, width):
    return nc.tensor.matmul(acc[:, b, 0:width], g.zeros[:, :], g.zeros[:, 0:1].broadcast_to([P, width]),
                            start=True, stop=True, skip_group_check=True)


def close_bank(nc, g, acc, b):
    return nc.tensor.matmul(acc[:, b, 0:2], g.zeros[:, :], g.zeros[:, 0:2], start=False, stop=True,
                            skip_group_check=True)


def attend_four(nc, sem, g, layer):
    H, W, PH, PASSES = 4, F // 4 + 1, 2, 2
    W3 = PIECES * W
    PAIR = 4 * W3
    R, LT = 1024, 4
    NB = R // P
    BLOCKS = N // R
    SUB = R // IBLK
    STEPS_ITER = 2 * LT
    LOOPS = T // STEPS_ITER
    STEPS = T
    BUFS = 4
    WIDE = PH * R
    HELD = 2 * LT
    adj_in = [sem("adj_in0"), sem("adj_in1")]
    row_in = [sem("row_in0"), sem("row_in1")]
    signs, masks, used = sem("signs"), sem("masks"), sem("used")
    acc_ready, acc_free, sums_used, chain = sem("acc_ready"), sem("acc_free"), sem("sums_used"), sem("chain")
    stood = sem("stood")
    with ExitStack() as st:
        def sb(name, shape, dt=F32):
            return st.enter_context(nc.sbuf_tensor(f"{name}_{layer}", shape, dt))

        adj = [sb(f"adj{q}", [P, SUB, LT, IBLK], BF16) for q in range(2)]
        row = [sb(f"row{q}", [P, PH, R]) for q in range(2)]
        sgn = [sb(f"sgn{q}", [P, WIDE], BF16) for q in range(BUFS)]
        mask = [sb(f"mask{q}", [P, WIDE], BF16) for q in range(BUFS)]
        acc = st.enter_context(nc.psum_tensor(f"acc_{layer}", [P, 8, BANK], F32))
        raw = sb("raw", [P, 8, PAIR])
        tot = sb("tot", [P, NB * 4, W])
        res, tmp = sb("res", [P, NB * PH, W]), sb("tmp", [P, NB * PH, W])
        flag = sb("flag", [P, NB * PH])
        with nc.Block() as block:

            @block.sync
            def _(sp):
                for ps in range(PASSES):
                    with sp.Fori(0, BLOCKS // 2) as bb:
                        for par in range(2):
                            blk = bb * 2 + par
                            done = ps * BLOCKS
                            sp.wait_ge(signs, (blk + (done + 1)) * STEPS)
                            src = g.rows1[ps * PH:(ps + 1) * PH, bass.ds(blk * R, R)]
                            sp.dma_start(row[par][:, :, :], src.unsqueeze(0).broadcast_to([P, PH, R])).then_inc(row_in[par], 16)
                            with sp.Fori(0, LOOPS) as j:
                                for q in range(2):
                                    load = ((blk + done) * LOOPS + j) * 2 + q
                                    sp.wait_ge(used, (load + 1) * LT)
                                    src = g.adj_t[bass.ds(blk * SUB, SUB), :, bass.ds((j * 2 + q) * LT, LT), :]
                                    src = src.rearrange("s p t i -> p s t i")
                                    sp.dma_start(adj[q][:, :, :, :], src).then_inc(adj_in[q], 16)

            @block.scalar
            def _(act):
                act.sem_inc(signs, 2 * STEPS)
                for ps in range(PASSES):
                    with act.Fori(0, BLOCKS // 2) as bb:
                        for par in range(2):
                            blk = bb * 2 + par + ps * BLOCKS
                            act.wait_ge(row_in[par], (bb + (ps * (BLOCKS // 2) + 1)) * 16)
                            with act.Fori(0, LOOPS) as j:
                                for k in range(STEPS_ITER):
                                    n = (blk * LOOPS + j) * STEPS_ITER + k
                                    act.wait_ge(masks, n + 1)
                                    for h in range(PH):
                                        col = (j * STEPS_ITER + k) * H + (ps * PH + h)
                                        last = nc.scalar.activation(sgn[k % BUFS][:, h * R:(h + 1) * R], row[par][:, h, :],
                                                                    ACT.Sign, bias=g.score[:, bass.ds(col, 1)])
                                    last.then_inc(signs, 1)

            @block.vector
            def _(dve):
                dve.sem_inc(masks, BUFS)

                def steps(it, evacuate=None):
                    for k in range(STEPS_ITER):
                        n = it * STEPS_ITER + k
                        q, kk = k // LT, k % LT
                        if kk == 0:
                            dve.wait_ge(adj_in[q], (it + 1) * 16)
                        dve.wait_ge(signs, n + (1 + 2 * STEPS))
                        dve.wait_ge(used, n + (1 + HELD - BUFS))
                        x = sgn[k % BUFS][:, :].rearrange("p (h s i) -> p h s i", h=PH, s=SUB)
                        m = mask[k % BUFS][:, :].rearrange("p (h s i) -> p h s i", h=PH, s=SUB)
                        a = adj[q][:, :, kk, :].unsqueeze(1).broadcast_to([P, PH, SUB, IBLK])
                        nc.vector.tensor_tensor(m, x, a, ALU.is_equal).then_inc(masks, 1)
                        if k == BUFS - 2 and evacuate:
                            evacuate()

                def sums_out(blk):
                    dve.wait_ge(sums_used, blk + 1)
                    for b in range(8):
                        dve.wait_ge(acc_ready, blk * 8 + (b + 1))
                        nc.vector.tensor_copy(raw[:, b, :], acc[:, b, 0:PAIR]).then_inc(acc_free, 1)

                with dve.Fori(0, PASSES * BLOCKS) as blk:
                    steps(blk * LOOPS, lambda: sums_out(blk))
                    with dve.Fori(1, LOOPS) as j:
                        steps(blk * LOOPS + j)
                sums_out(PASSES * BLOCKS)

            @block.tensor
            def _(pe):
                pe.sem_inc(used, HELD)
                for b in range(8):
                    zero_bank(nc, g, acc, b, PAIR).then_inc(acc_ready, 1)
                for ps in range(PASSES):
                    with pe.Fori(0, BLOCKS) as bb:
                        blk = bb + ps * BLOCKS

                        def steps(j, opening=False):
                            for k in range(STEPS_ITER):
                                n = (blk * LOOPS + j) * STEPS_ITER + k
                                pe.wait_ge(masks, n + (1 + BUFS))
                                first = opening and k == 0
                                at = (j * STEPS_ITER + k) * (2 * PAIR) + ps * PAIR
                                for b in range(NB):
                                    if first:
                                        pe.wait_ge(acc_free, blk * 8 + (b + 1))
                                    for h in range(PH):
                                        nc.tensor.matmul(acc[:, b, h * 2 * W3:(h + 1) * 2 * W3],
                                                         mask[k % BUFS][:, h * R + b * P:h * R + (b + 1) * P],
                                                         g.split[:, bass.ds(at + h * 2 * W3, 2 * W3)],
                                                         start=first and h == 0, stop=False, skip_group_check=True)
                                    i = b * P % IBLK
                                    last = nc.tensor.matmul(acc[:, b, W3:3 * W3], adj[k // LT][:, b * P // IBLK, k % LT, i:i + P],
                                                            g.split[:, bass.ds(at + W3, 2 * W3)],
                                                            start=False, stop=False, skip_group_check=True)
                                last.then_inc(used, 1)

                        steps(0, opening=True)
                        with pe.Fori(1, LOOPS) as j:
                            steps(j)
                        for b in range(8):
                            close_bank(nc, g, acc, b).then_inc(acc_ready, 1)

            @block.gpsimd
            def _(pool):
                pool.sem_inc(sums_used, 1)
                pool.wait_ge(acc_free, 8)
                pool.sem_inc(sums_used, 1)
                LINKS = 7
                each = 16 if layer < 3 else 16 * PH
                before = g.pool_stores
                g.pool_stores += each * PASSES * BLOCKS
                for ps in range(PASSES):
                    with pool.Fori(0, BLOCKS) as bb:
                        blk = bb + ps * BLOCKS
                        made = [0]

                        def link(ins):
                            made[0] += 1
                            ins.then_inc(chain, 1)
                            pool.wait_ge(chain, blk * LINKS + made[0])

                        def heads(v):
                            return v.rearrange("p (b h) w -> p b h w", h=PH)

                        def factor(v):
                            v = v[:, bass.ds(bb * (NB * H), NB * H)].rearrange("p (b h) -> p b h", h=H)
                            return v[:, :, ps * PH:(ps + 1) * PH].unsqueeze(3).broadcast_to([P, NB, PH, W])

                        pool.wait_ge(acc_free, blk * 8 + 16)
                        r = raw[:, :, :].rearrange("p b (c q w) -> p (b c) q w", c=4, q=PIECES)
                        link(nc.gpsimd.tensor_tensor(tot[:, :, :], r[:, :, 0, :], r[:, :, 1, :], ALU.add))
                        nc.gpsimd.tensor_tensor(tot[:, :, :], tot[:, :, :], r[:, :, 2, :], ALU.add).then_inc(sums_used, 1)
                        pool.wait_ge(sums_used, blk + 3)
                        four = tot[:, :, :].rearrange("p (b c) w -> p b c w", c=4)
                        link(nc.gpsimd.tensor_tensor(heads(res[:, :, :]), four[:, :, 0:4:3, :], factor(g.rb), ALU.mult))
                        link(nc.gpsimd.tensor_tensor(heads(tmp[:, :, :]), four[:, :, 1:3, :], factor(g.ra), ALU.mult))
                        link(nc.gpsimd.tensor_tensor(res[:, :, :], res[:, :, :], tmp[:, :, :], ALU.subtract))
                        pool.sem_inc(stood, 1)
                        link(nc.gpsimd.tensor_scalar(flag[:, :], res[:, :, W - 1], 0.0, None, ALU.is_equal))
                        cs = g.colsum[:, ps * PH * W:(ps + 1) * PH * W]
                        cs = cs.rearrange("p (h w) -> p h w", h=PH).unsqueeze(1).broadcast_to([P, NB, PH, W])
                        fl = flag[:, :].rearrange("p (b h) -> p b h", h=PH).unsqueeze(3).broadcast_to([P, NB, PH, W])
                        link(nc.gpsimd.tensor_tensor(heads(tmp[:, :, :]), fl, cs, ALU.mult))
                        link(nc.gpsimd.tensor_tensor(res[:, :, :], res[:, :, :], tmp[:, :, :], ALU.add))
                        if layer < 3:
                            dst = g.sums[layer][bass.ds(bb * NB, NB), :, ps * PH * W:(ps + 1) * PH * W]
                            pool.dma_start(dst.rearrange("b p w -> p b w"),
                                           res[:, :, :].rearrange("p (b h) w -> p b (h w)", h=PH)).then_inc(g.pool_stored, 16)
                        else:
                            for h in range(PH):
                                dst = g.sums[layer][ps * PH + h, bass.ds(bb * R, R), :]
                                pool.dma_start(dst.rearrange("(b p) w -> p b w", p=P),
                                               heads(res[:, :, :])[:, :, h, :]).then_inc(g.pool_stored, 16)
                        pool.wait_ge(g.pool_stored, (blk + 1) * each + before)
                        pool.sem_inc(stood, 1)


def gat_kernel(nc, x, adj, L0_W, L0_a1, L0_a2, L1_W, L1_a, L2_W, L2_a, L3_W, L3_a, out):
    D = F // 4
    one = lambda v: v.rearrange("(h d) -> h d", h=1)
    weights = [
        (L0_W, one(L0_a1), one(L0_a2)),
        (L1_W, L1_a[0, :, 0:D], L1_a[0, :, D:2 * D]),
        (L2_W, L2_a[0:F, :].rearrange("d h -> h d"), L2_a[F:2 * F, :].rearrange("d h -> h d")),
        (L3_W, L3_a[:, D:2 * D, 0], L3_a[:, 0:D, 0]),
    ]
    with ExitStack() as ctx:
        ctx.enter_context(nc.allow_non_contiguous_dma("weights"))
        g = tensors(nc, ctx)
        with stage_semaphores(nc, "setup") as sem:
            setup(nc, sem, g, weights)
        with ExitStack() as factored:
            g.split = factored.enter_context(nc.sbuf_tensor("split", [P, T * STAT_MAX], BF16))
            for layer in range(4):
                with stage_semaphores(nc, f"nodes{layer}") as sem:
                    update_nodes(nc, sem, g, layer, x, out)
                with stage_semaphores(nc, f"attend{layer}") as sem:
                    if layer == 0:
                        attend_and_transpose(nc, sem, g, adj)
                    elif KINDS[layer].heads == 1:
                        attend_one(nc, sem, g, layer)
                    else:
                        attend_four(nc, sem, g, layer)
            with stage_semaphores(nc, "nodes4") as sem:
                update_nodes(nc, sem, g, 4, x, out)
        with stage_semaphores(nc, "decide") as sem:
            decide(nc, sem, g)
        go = nc.values_load(g.exact[0:1, 0:1], min_val=0, max_val=1)
        for layer in range(4):
            with stage_semaphores(nc, f"xnodes{layer}") as sem:
                update_nodes(nc, sem, g, layer, x, out, go)
            with stage_semaphores(nc, f"xattend{layer}") as sem:
                attend_exact(nc, sem, g, layer, adj, go)
        with stage_semaphores(nc, "xnodes4") as sem:
            update_nodes(nc, sem, g, 4, x, out, go)


_INS = ["x", "adj", "L0_gnn_W", "L0_gnn_a1", "L0_gnn_a2", "L1_gnn_W", "L1_gnn_a", "L2_gnn_W", "L2_gnn_a",
        "L3_gnn_W", "L3_gnn_a"]


def kernel(**inputs):
    import numpy as _np
    import concourse.bacc as _bacc
    from concourse import mybir as _mybir
    from concourse.bass_utils import run_bass_kernel_spmd as _run

    nc = _bacc.Bacc("TRN2", target_bir_lowering=False, num_devices=1)
    arrays, args = {}, []
    for name in _INS:
        a = _np.ascontiguousarray(inputs[name])
        arrays[f"in_{name}"] = a
        args.append(nc.dram_tensor(f"in_{name}", a.shape, _mybir.dt.from_np(a.dtype), kind="ExternalInput").ap())
    args.append(nc.dram_tensor("out_nodes", (N, F), F32, kind="ExternalOutput").ap())
    gat_kernel(nc, *args)
    r = _run(nc, [arrays], core_ids=[0])
    return r.results[0]["out_nodes"]
```
